# Optimizing a Trainium2 kernel written in Bass

```python
import numpy as np
import jax
import jax.numpy as jnp

def _softmax(x, axis=-1):
    return jax.nn.softmax(x, axis=axis)

def _gelu(x):
    return jax.nn.gelu(x, approximate=True)

def _silu(x):
    return jax.nn.silu(x)

def _sigmoid(x):
    return jax.nn.sigmoid(x)

def _layernorm(x, axis=-1, eps=1e-05):
    m = jnp.mean(x, axis=axis, keepdims=True)
    v = jnp.var(x, axis=axis, keepdims=True)
    return (x - m) / jnp.sqrt(v + eps)

def _scatter_add(tgt, idx, src, axis=0):
    return tgt.at[idx].add(src)

def _segment_sum(src, seg, n):
    return jax.ops.segment_sum(src, seg, n)
kernel_name = 'mk_gnn_preln_d2_gnn_r8_225e76'

def setup_inputs(seed: int=0):
    np.random.seed(seed)
    _w = jnp.asarray

    def _rec_inputs():
        import jax
        import jax.numpy as jnp
        _gk = jax.random.key(seed)
        x = -0.0003713 + 1 * jax.random.normal(jax.random.fold_in(_gk, 1), (6250, 256), jnp.float32)
        src = jax.random.randint(jax.random.fold_in(_gk, 2), (200000,), 0, 6250, jnp.int32)
        dst = jax.random.randint(jax.random.fold_in(_gk, 3), (200000,), 0, 6250, jnp.int32)
        _o = jnp.argsort(dst, stable=True)
        src = src[_o]
        dst = dst[_o]
        edge_attr_96 = -4.21973e-05 + 0.999841 * jax.random.normal(jax.random.fold_in(_gk, 12), (200000, 96), jnp.float32)
        return (x, src, dst, edge_attr_96)
    x, src, dst, edge_attr_96 = _rec_inputs()

    def _L0_gnn_setup():
        import jax, jax.numpy as jnp
        import numpy as np
        N = 6250
        E = 100000
        D_IN = 256
        D_H = 512
        D_OUT = 256
        key = jax.random.key(seed)
        ks = jax.random.split(key, 12)
        s = lambda d: 1.0 / np.sqrt(d)
        x = jax.random.normal(ks[0], (N, D_IN), dtype=jnp.float32)
        edge_index = jax.random.randint(ks[1], (2, E), 0, N, dtype=jnp.int64)
        W_rel = jax.random.uniform(ks[2], (D_IN, D_H), jnp.float32, -s(D_IN), s(D_IN))
        b_rel = jax.random.uniform(ks[3], (D_H,), jnp.float32, -s(D_IN), s(D_IN))
        W_root = jax.random.uniform(ks[4], (D_IN, D_H), jnp.float32, -s(D_IN), s(D_IN))
        W_ih = jax.random.uniform(ks[5], (4 * D_H, D_H), jnp.float32, -s(D_H), s(D_H))
        W_hh = jax.random.uniform(ks[6], (4 * D_H, D_H), jnp.float32, -s(D_H), s(D_H))
        b_ih = jax.random.uniform(ks[7], (4 * D_H,), jnp.float32, -s(D_H), s(D_H))
        b_hh = jax.random.uniform(ks[8], (4 * D_H,), jnp.float32, -s(D_H), s(D_H))
        W_fc = jax.random.uniform(ks[9], (D_H, D_OUT), jnp.float32, -s(D_H), s(D_H))
        b_fc = jax.random.uniform(ks[10], (D_OUT,), jnp.float32, -s(D_H), s(D_H))
        return {'x': x, 'edge_index': edge_index, 'W_rel': W_rel, 'b_rel': b_rel, 'W_root': W_root, 'W_ih': W_ih, 'W_hh': W_hh, 'b_ih': b_ih, 'b_hh': b_hh, 'W_fc': W_fc, 'b_fc': b_fc}
    _L0_gnn_all = _L0_gnn_setup()
    _L0_gnn_in = {k: v for k, v in _L0_gnn_all.items() if k in ('W_rel', 'b_rel', 'W_root', 'W_ih', 'W_hh', 'b_ih', 'b_hh', 'W_fc', 'b_fc')}
    del _L0_gnn_all

    def _L1_gnn_setup():
        import jax, jax.numpy as jnp
        import numpy as np
        N_NODES = 6250
        N_EDGES = 100000
        EDGE_F = 96
        NODE_F = 256
        GLOB_F = 64
        HIDDEN = 1024
        N_GRAPHS = 8
        MLP_IN = NODE_F + 3 * EDGE_F + GLOB_F
        key = jax.random.key(seed)
        ks = jax.random.split(key, 9)
        x = jax.random.normal(ks[0], (N_NODES, NODE_F), dtype=jnp.float32)
        edge_attr = jax.random.normal(ks[1], (N_EDGES, EDGE_F), dtype=jnp.float32)
        u = jax.random.normal(ks[2], (N_GRAPHS, GLOB_F), dtype=jnp.float32)
        W1 = jax.random.normal(ks[3], (MLP_IN, HIDDEN), dtype=jnp.float32) * (1.0 / np.sqrt(MLP_IN))
        b1 = jax.random.normal(ks[4], (HIDDEN,), dtype=jnp.float32) * 0.01
        W2 = jax.random.normal(ks[5], (HIDDEN, NODE_F), dtype=jnp.float32) * (1.0 / np.sqrt(HIDDEN))
        b2 = jax.random.normal(ks[6], (NODE_F,), dtype=jnp.float32) * 0.01
        edge_index = jax.random.randint(ks[7], (2, N_EDGES), 0, N_NODES, dtype=jnp.int64 if jax.config.jax_enable_x64 else jnp.int32)
        batch = jnp.sort(jax.random.randint(ks[8], (N_NODES,), 0, N_GRAPHS, dtype=jnp.int32))
        return {'x': x, 'edge_attr': edge_attr, 'u': u, 'W1': W1, 'b1': b1, 'W2': W2, 'b2': b2, 'edge_index': edge_index, 'batch': batch}
    _L1_gnn_all = _L1_gnn_setup()
    _L1_gnn_in = {k: v for k, v in _L1_gnn_all.items() if k in ('u', 'W1', 'b1', 'W2', 'b2')}
    del _L1_gnn_all
    return {'x': x, 'src': src, 'dst': dst, 'edge_attr_96': edge_attr_96, 'L0_gnn_W_rel': _L0_gnn_in['W_rel'], 'L0_gnn_b_rel': _L0_gnn_in['b_rel'], 'L0_gnn_W_root': _L0_gnn_in['W_root'], 'L0_gnn_W_ih': _L0_gnn_in['W_ih'], 'L0_gnn_W_hh': _L0_gnn_in['W_hh'], 'L0_gnn_b_ih': _L0_gnn_in['b_ih'], 'L0_gnn_b_hh': _L0_gnn_in['b_hh'], 'L0_gnn_W_fc': _L0_gnn_in['W_fc'], 'L0_gnn_b_fc': _L0_gnn_in['b_fc'], 'L1_gnn_u': _L1_gnn_in['u'], 'L1_gnn_W1': _L1_gnn_in['W1'], 'L1_gnn_b1': _L1_gnn_in['b1'], 'L1_gnn_W2': _L1_gnn_in['W2'], 'L1_gnn_b2': _L1_gnn_in['b2']}

def reference(x, src, dst, edge_attr_96, L0_gnn_W_rel, L0_gnn_b_rel, L0_gnn_W_root, L0_gnn_W_ih, L0_gnn_W_hh, L0_gnn_b_ih, L0_gnn_b_hh, L0_gnn_W_fc, L0_gnn_b_fc, L1_gnn_u, L1_gnn_W1, L1_gnn_b1, L1_gnn_W2, L1_gnn_b2):
    import jax
    import jax.numpy as jnp

    def _L0_gnn_ref(x, edge_index, W_rel, b_rel, W_root, W_ih, W_hh, b_ih, b_hh, W_fc, b_fc):
        import jax, jax.numpy as jnp
        import numpy as np
        N = 6250
        E = 100000
        D_IN = 256
        D_H = 512
        D_OUT = 256
        src, dst = (edge_index[0], edge_index[1])
        agg = jax.ops.segment_sum(x[src], dst, num_segments=N)
        h = jax.nn.relu(agg @ W_rel + b_rel + x @ W_root)
        gates = h @ W_ih.T + b_ih + b_hh
        i, f, g, o = jnp.split(gates, 4, axis=-1)
        c = jax.nn.sigmoid(i) * jnp.tanh(g)
        h_lstm = jax.nn.sigmoid(o) * jnp.tanh(c)
        return h_lstm @ W_fc + b_fc

    def _L1_gnn_ref(x, edge_attr, u, W1, b1, W2, b2, edge_index, batch):
        import jax, jax.numpy as jnp
        import numpy as np
        N_NODES = 6250
        N_EDGES = 100000
        EDGE_F = 96
        NODE_F = 256
        GLOB_F = 64
        HIDDEN = 1024
        N_GRAPHS = 8
        MLP_IN = NODE_F + 3 * EDGE_F + GLOB_F
        col = edge_index[1]
        n = x.shape[0]
        out1 = jax.ops.segment_sum(edge_attr, col, num_segments=n)
        cnt = jax.ops.segment_sum(jnp.ones((edge_attr.shape[0], 1), edge_attr.dtype), col, num_segments=n)
        out2 = jax.ops.segment_max(edge_attr, col, num_segments=n)
        out2 = jnp.where(cnt > 0, out2, jnp.zeros_like(out2))
        out3 = out1 / jnp.maximum(cnt, 1.0)
        h = jnp.concatenate([x, out1, out2, out3, u[batch]], axis=1)
        h = jax.nn.relu(h @ W1 + b1) @ W2 + b2
        return h + x
    edge_index = jnp.stack([src, dst])
    batch0 = jnp.zeros((6250,), jnp.int32)
    h = jnp.maximum(_layernorm(x, axis=-1), 0.0)
    x = x + _L0_gnn_ref(h, edge_index, L0_gnn_W_rel, L0_gnn_b_rel, L0_gnn_W_root, L0_gnn_W_ih, L0_gnn_W_hh, L0_gnn_b_ih, L0_gnn_b_hh, L0_gnn_W_fc, L0_gnn_b_fc)
    h = jnp.maximum(_layernorm(x, axis=-1), 0.0)
    x = x + _L1_gnn_ref(h, edge_attr_96, L1_gnn_u, L1_gnn_W1, L1_gnn_b1, L1_gnn_W2, L1_gnn_b2, edge_index, batch0)
    return x

_drawn_inputs = setup_inputs


def setup_inputs(seed=0):
    import zlib

    import numpy as np

    out = dict(_drawn_inputs(seed))
    spreads = {}
    factors = {'L0_gnn_b_rel': 63.194,
     'L0_gnn_W_root': 5.49,
     'L0_gnn_b_ih': 35.748,
     'L0_gnn_b_hh': 30.944,
     'L0_gnn_b_fc': 3.12,
     'L1_gnn_b1': 8.0,
     'L1_gnn_b2': 8.0}
    for name, (base, spread) in spreads.items():
        noise = np.random.default_rng([zlib.crc32(name.encode()), seed]).standard_normal(out[name].shape)
        drawn = base * np.exp(spread * noise) if base else spread * noise
        out[name] = jnp.asarray(drawn.astype(out[name].dtype))
    for name, factor in factors.items():
        out[name] = (out[name] * factor).astype(out[name].dtype)
    return out
```

```python
import concourse.bass as bass
from concourse import mybir
from contextlib import ExitStack

N, E = 6250, 200000
D, F, H, G3, Z = 256, 96, 512, 3, 1024
P = 128
NT = -(-N // P)
NPAD = NT * P
J = 8
UNIT = P * J
NU = -(-E // UNIT)
UPI = 4
EPAD = NU * UNIT
K = 30
NR = 2
SB = 400
NB = E // SB
LNG = 7
RING = 4
BANKS = 3
HSCALE = 1024.0
BIG = 3.0e38
EPS = 1e-5
FAR = 10000000.0
PAIRS = NU + NT
assert NU == UPI * NT and NT % LNG == 0 and E % SB == 0


def build(nc, x, src, dst, edge, wrel, brel, wroot, wih, bih, bhh, wfc, bfc, u0, w1, b1, w2, b2, out):
    f32, f16, i32, i16, u32 = (mybir.dt.float32, mybir.dt.float16, mybir.dt.int32, mybir.dt.int16,
                               mybir.dt.uint32)
    ALU, ACT, AX = mybir.AluOpType, mybir.ActivationFunctionType, mybir.AxisListType
    ds = bass.ds

    hsplit = nc.dram_tensor("hsplit", (NPAD, 2 * D), f16).ap()

    with ExitStack() as ctx:
        def sb(name, shape, dt):
            return ctx.enter_context(nc.sbuf_tensor(name, shape, dt))

        def pb(name, shape, dt):
            return ctx.enter_context(nc.psum_tensor(name, shape, dt))

        def sem(name):
            return ctx.enter_context(nc.semaphore(name))

        Wrel = sb("Wrel", [P, 2, H], f32)
        Wroot = sb("Wroot", [P, 2, H], f32)
        Wih = sb("Wih", [P, 4, G3, H], f32)
        Wfc = sb("Wfc", [P, 4, D], f32)
        W1h = sb("W1h", [P, 2, Z], f32)
        W1e = sb("W1e", [F, 3, Z], f32)
        W2 = sb("W2", [P, 8, D], f32)
        brel_c = sb("brel_c", [P, 4], f32)
        gb = sb("gb", [P, 16], f32)
        gb2 = sb("gb2", [P, 16], f32)
        b1_c = sb("b1_c", [P, 8], f32)
        bfc_r = sb("bfc_r", [P, D], f32)
        b2_r = sb("b2_r", [P, D], f32)
        u_c = sb("u_c", [64, 1], f32)
        ident = sb("ident", [P, P], f32)
        node = sb("node", [P, NT], f32)
        base = sb("base", [P, NT + 1], f32)
        col = sb("col", [P, P], f32)
        dtab = sb("dtab", [P, NU * J], i16)
        sidx = sb("sidx", [P, UPI, J], u32)
        start = sb("start", [P, NT + 1], f32)
        end = sb("end", [P, NT], f32)
        hasany = sb("hasany", [P, NT], f32)
        rcnt = sb("rcnt", [P, NT], f32)
        blk = sb("blk", [P, NT], f32)
        blku = sb("blku", [P, NT], u32)
        blo = sb("blo", [P, NR, NT], f32)
        bhi = sb("bhi", [P, NR, NT], f32)
        brow = sb("brow", [P, NR, NT], u32)
        bnow = sb("bnow", [P, NR], u32)
        tab = sb("tab", [1, NU + 1], i32)
        flags = sb("flags", [1, 2], i32)
        agg = sb("agg", [P, NT + 1, D], f32)
        rows = [sb(f"rows{q}", [P, J, 2 * D], f16) for q in range(2)]
        hot = sb("hot", [P, RING, J, P], f16)
        xblk = [sb(f"xblk{r}", [P, K, F], f32) for r in range(NR)]
        xneg = sb("xneg", [P, K, F], f32)
        mask = sb("mask", [P, NR, K], f32)
        neg = sb("neg", [P, NR, K], f32)
        part = sb("part", [P, 2, 2, F], f32)
        feat = sb("feat", [P, 3, F], f32)
        xa = sb("xa", [P, D], f32)
        aggs = sb("aggs", [P, D], f32)
        ahT = sb("ahT", [P, 4, P], f32)
        h1T = sb("h1T", [P, 4, P], f32)
        gio = sb("gio", [P, G3, 4, P], f32)
        hlT = sb("hlT", [P, 4, P], f32)
        xf = sb("xf", [P, D], f32)
        x2 = sb("x2", [P, D], f32)
        h2 = sb("h2", [P, D], f32)
        h2T = sb("h2T", [P, 2, P], f32)
        featT = sb("featT", [F, 3, P], f32)
        zT = sb("zT", [P, 8, P], f32)
        ob = sb("ob", [P, D], f32)
        rs = sb("rs", [P, NT], f32)
        nm = sb("nm", [P, NT], f32)
        st = sb("st", [P, LNG, 6], f32)
        mv = sb("mv", [P, LNG, 2], f32)
        lna = sb("lna", [P, LNG], f32)
        lnb = sb("lnb", [P, LNG], f32)
        lny = sb("lny", [P, LNG], f32)
        rs2 = sb("rs2", [P, 1], f32)
        nm2 = sb("nm2", [P, 1], f32)
        aflat = agg[:, :, :].rearrange("p t d -> p (t d)")
        GX = LNG * D
        xg = [aflat[:, q * GX:(q + 1) * GX].rearrange("p (t d) -> p t d", t=LNG) for q in range(2)]
        hg = [aflat[:, (2 + q) * GX:(3 + q) * GX].rearrange("p (t d) -> p t d", t=LNG) for q in range(2)]
        hs = [aflat[:, (4 + q) * GX:(5 + q) * GX].bitcast(f16).rearrange("p (t d) -> p t d", t=LNG)
              for q in range(2)]
        SLOTS = 7
        fine = [xblk[0][:, :, :].rearrange("p k f -> p (k f)")[:, q * SB:(q + 1) * SB].bitcast(i32)
                for q in range(SLOTS)]
        x1f = xblk[1][:, :, :].rearrange("p k f -> p (k f)")
        ends_b = x1f[:, 0:NB]
        junk = x1f[:, NB:2 * NB]
        erow = x1f[0:1, 2 * NB:3 * NB]
        erow_i = x1f[0:1, 3 * NB:4 * NB].bitcast(i32)
        d32 = xneg[:, :, :].rearrange("p k f -> p (k f)")[:, 0:NU * J].bitcast(i32)
        xneg_row = xneg[:, :, :].rearrange("p k f -> p (k f)")
        cmp = aflat[0:1, 0:NU * NT].rearrange("p (u t) -> p u t", u=NU)
        tabf = xneg_row[0:1, 2048:2048 + NU + 1]
        lim = xneg_row[0:1, 1600:1600 + NU]
        limt = xneg_row[0:1, 1800:1800 + NT]
        cmpt = xneg_row[0:1, 1900:1900 + NT]
        mrow = xneg_row[0:1, 2300:2300 + P]
        fl = xneg_row[0:1, 2500:2506]
        cntt = xneg_row[:, 2600:2600 + NT]
        mcnt = xneg_row[:, 2700:2701]
        browf = xneg_row[:, 2720:2720 + NT]
        rcnt_tmp = xneg_row[:, 2780:2780 + NT]
        shA = hot[:, 0, :, :].rearrange("p j n -> p (j n)").bitcast(f32)[:, 0:P]
        shB = hot[:, 1, :, :].rearrange("p j n -> p (j n)").bitcast(f32)[:, 0:P]
        w1u = rows[0][0:64, :, :].rearrange("p j n -> p (j n)").bitcast(f32)[:, 0:Z]
        ones1 = rows[1][0:1, 0, 0:2 * P].bitcast(f32)
        rx = mask[:, 0, 0:8]
        rxu = mask[:, 1, 0:1].bitcast(u32)

        acc = pb("acc", [P, BANKS, 512], f32)
        pTA = pb("pTA", [P, 4, P], f32)
        pT23 = pb("pT23", [P, 512], f32)
        pF = pb("pF", [P, 512], f32)
        pB = [pb(f"pB{q}", [P, 4, P], f32) for q in range(2)]
        pFE, pT2 = pF[:, 0:D], pT23[:, 0:D]

        l_w, l_x, l_d, l_e, l_c = sem("l_w"), [sem("l_x0"), sem("l_x1")], sem("l_d"), sem("l_e"), sem("l_c")
        consts = sem("consts")
        pd = sem("pd")
        erow_ready, ends_ready, ends_copied = sem("erow_ready"), sem("ends_ready"), sem("ends_copied")
        coarse_ready = sem("coarse_ready")
        fine_in = [sem(f"fine_in{q}") for q in range(SLOTS)]
        fine_used = sem("fine_used")
        start_ready, shifted, bias_mm = sem("start_ready"), sem("shifted"), sem("bias_mm")
        mcnt_ready, mcnt_T, pro_done = sem("mcnt_ready"), sem("mcnt_T"), sem("pro_done")
        ln_stats, ln_h, ln_split = sem("ln_stats"), sem("ln_h"), sem("ln_split")
        h_out = [sem("h_out0"), sem("h_out1")]
        tab_ready = sem("tab_ready")
        lnchain = sem("lnchain")
        idx_in = [sem(f"idx_in{q}") for q in range(UPI)]
        rows_in = [sem("rows_in0"), sem("rows_in1")]
        hot_ready, pair_done, added = sem("hot_ready"), sem("pair_done"), sem("added")
        bidx = sem("bidx")
        blk_in = [sem("blk_in0"), sem("blk_in1")]
        blk_used = [sem("blk_used0"), sem("blk_used1")]
        mask_ready, neg_done, neg_used, feat_ready = sem("mask_ready"), sem("neg_done"), sem("neg_used"), sem("feat_ready")
        fchain = sem("fchain")
        mchain = sem("mchain")
        xa_in, xf_in, stored = sem("xa_in"), sem("xf_in"), sem("stored")
        sc_hg = sem("sc_hg")
        sc_h, te_T, sc_T, te_A, sc_A = sem("sc_h"), sem("te_T"), sem("sc_T"), sem("te_A"), sem("sc_A")
        te_B, sc_B, ve_c, sc_tc, ve_hl = sem("te_B"), sem("sc_B"), sem("ve_c"), sem("sc_tc"), sem("ve_hl")
        te_FC, ve_x2, ve_ln, sc_h2, te_T2, sc_T2 = (sem("te_FC"), sem("ve_x2"), sem("ve_ln"), sem("sc_h2"),
                                                    sem("te_T2"), sem("sc_T2"))
        te_T3, sc_T3, te_D, sc_D, te_E, ve_res, ve_out = (sem("te_T3"), sem("sc_T3"), sem("te_D"), sem("sc_D"),
                                                          sem("te_E"), sem("ve_res"), sem("ve_out"))
        lchain, rchain, schain = sem("lchain"), sem("rchain"), sem("schain")
        r_idx, r_in, rdchain, r_feat = sem("r_idx"), sem("r_in"), sem("rdchain"), sem("r_feat")

        block = ctx.enter_context(nc.Block())

        ADDED0 = 2
        DONE0 = RING

        turn = sem("turn")

        def alone(eng):
            eng.sem_inc(turn, 1)

        def first(n):
            return isinstance(n, int) and n == 0

        def tile_of(ap, t):
            return ap[:, ds(t, 1)]

        def ended(eng, u):
            return eng.value_load(tab[0:1, ds(u, 1)], min_val=0, max_val=NT)

        def schedule(body):
            body(0, True, False, False, False)
            body(1, True, True, False, False)
            body(2, True, True, True, False)
            yield
            body(NT - 1, True, True, True, True)
            body(NT, False, True, True, True)
            body(NT + 1, False, False, True, True)
            body(NT + 2, False, False, False, True)

        def run(eng, body):
            steps = schedule(body)
            next(steps)
            with eng.Fori(3, NT - 1) as i:
                body(i, True, True, True, True)
            for _ in steps:
                pass

        @block.sync
        def _(sp):
            sp.dma_start(erow_i, dst[0:E].rearrange("(b s) -> s b", s=SB)[SB - 1:SB, :],
                         allow_slow_non_contiguous=True).then_inc(l_e, 16)
            for g in range(2):
                sp.dma_start(xg[g], x[g * LNG * P:(g + 1) * LNG * P, :].rearrange("(t p) d -> p t d", p=P)).then_inc(l_x[g], 16)
            sp.dma_start(d32.rearrange("p (u j) -> p u j", j=J), dst.rearrange("(u p j) -> p u j", p=P, j=J)).then_inc(l_d, 16)
            for q in range(UPI):
                sp.dma_start(sidx[:, q, :], src[q * UNIT:(q + 1) * UNIT, :].rearrange("(p j) o -> p (j o)", j=J)).then_inc(idx_in[q], 16)
            for g in range(2, NT // LNG):
                sp.wait_ge(ln_split, g - 1)
                sp.dma_start(xg[g % 2], x[g * LNG * P:(g + 1) * LNG * P, :].rearrange("(t p) d -> p t d", p=P)).then_inc(l_x[g % 2], 16)
            sp.dma_start(xa[:, :], x[0:P, :]).then_inc(xa_in, 16)
            sp.dma_start(xf[:, :], x[0:P, :]).then_inc(xf_in, 16)
            for dst_ap, src_ap in (
                (Wrel[:, :, :], wrel.rearrange("(k p) m -> p k m", p=P)),
                (Wroot[:, :, :], wroot.rearrange("(k p) m -> p k m", p=P)),
                (Wih[:, :, 0, :], wih[:, 0:H].rearrange("(k p) m -> p k m", p=P)),
                (Wih[:, :, 1, :], wih[:, 2 * H:3 * H].rearrange("(k p) m -> p k m", p=P)),
                (Wih[:, :, 2, :], wih[:, 3 * H:4 * H].rearrange("(k p) m -> p k m", p=P)),
                (Wfc[:, :, :], wfc.rearrange("(k p) m -> p k m", p=P)),
                (W1h[:, :, :], w1[0:D, :].rearrange("(k p) m -> p k m", p=P)),
                (W1e[:, :, :], w1[D:D + 3 * F, :].rearrange("(k p) m -> p k m", p=F)),
                (W2[:, :, :], w2.rearrange("(k p) m -> p k m", p=P)),
                (bfc_r[:, :], bfc.to_broadcast([P, D])),
                (b2_r[:, :], b2.to_broadcast([P, D])),
            ):
                sp.dma_start(dst_ap, src_ap).then_inc(l_w, 16)

            def body(i, units, T, B, E_):
                def next_sources(q):
                    if units and not (isinstance(i, int) and i == NT - 1):
                        sp.wait_ge(rows_in[q % 2], 16 * J * (2 * i + q // 2 + 1))
                        sp.dma_start(sidx[:, q, :], src[ds((i * UPI + UPI + q) * UNIT, UNIT), :]
                                     .rearrange("(p j) o -> p (j o)", j=J)).then_inc(idx_in[q], 16)

                next_sources(0)
                if E_:
                    sp.wait_ge(ve_out, i - 2)
                    sp.dma_start(out[ds((i - 3) * P, P), :], ob[:, :]).then_inc(stored, 16)
                next_sources(1)
                if T and not (isinstance(i, int) and i == NT):
                    sp.wait_ge(te_T, i)
                    sp.dma_start(xa[:, :], x[ds(i * P, P), :]).then_inc(xa_in, 16)
                next_sources(2)
                next_sources(3)
                if B and not (isinstance(i, int) and i == NT + 1):
                    sp.wait_ge(ve_x2, i - 1)
                    sp.dma_start(xf[:, :], x[ds((i - 1) * P, P), :]).then_inc(xf_in, 16)

            run(sp, body)

            redo = sp.value_load(flags[0:1, 0:1], min_val=0, max_val=1)
            sp.wait_ge(stored, 16 * NT)
            with sp.If(redo):
                with sp.Fori(0, NT) as t:
                    sp.wait_ge(te_T, t + NT)
                    sp.wait_ge(ve_out, t + NT)
                    sp.dma_start(xa[:, :], x[ds(t * P, P), :]).then_inc(xa_in, 16)
                    sp.dma_start(xf[:, :], x[ds(t * P, P), :]).then_inc(xf_in, 16)
                    sp.wait_ge(ve_out, t + NT + 1)
                    sp.dma_start(out[ds(t * P, P), :], ob[:, :]).then_inc(stored, 16)
                    sp.wait_ge(stored, (t + NT + 1) * 16)
                    alone(sp)

        @block.gpsimd
        def _(pool):
            def const(ins):
                ins.then_inc(consts, 1)

            const(nc.gpsimd.iota(node[:, :], [[P, NT]], 0, 1, allow_small_or_imprecise_dtypes=True))
            const(nc.gpsimd.iota(base[:, :], [[P, NT + 1]], 0, 0, allow_small_or_imprecise_dtypes=True))
            const(nc.gpsimd.iota(col[:, :], [[1, P]], 0, 0, allow_small_or_imprecise_dtypes=True))
            const(nc.gpsimd.memset(ident[:, :], 0.0))
            const(nc.gpsimd.memset(shA, 0.0))
            const(nc.gpsimd.memset(shB, 0.0))
            const(nc.gpsimd.memset(ones1, 1.0))
            const(nc.gpsimd.iota(lim, [[UNIT, NU]], UNIT, 0, allow_small_or_imprecise_dtypes=True))
            pool.wait_ge(consts, 8)
            for ap, off in ((ident[:, :], 0), (shA, -1), (shB, P - 1)):
                const(nc.gpsimd.affine_select(out=ap, in_=ap, compare_op=ALU.not_equal, fill=1.0, base=off,
                                              pattern=[[-1, P]], channel_multiplier=1))
            drows = dst[0:E].rearrange("(b s) -> b s", s=SB)
            for t in range(NT):
                pool.wait_ge(coarse_ready, t + 1)
                if t >= SLOTS:
                    pool.wait_ge(fine_used, t - SLOTS + 1)
                pool.indirect_dma_start(fine[t % SLOTS], None, drows,
                                        bass.IndirectOffsetOnAxis(ap=blku[:, t:t + 1], axis=0),
                                        bounds_check=NB - 1, oob_is_err=False).then_inc(fine_in[t % SLOTS], 16)

            pool.wait_ge(tab_ready, 1)
            for q in range(2):
                pool.wait_ge(h_out[q], 16 * ((NT // LNG + 1 - q) // 2))

            def gather_blocks(r, f):
                if not first(f):
                    pool.wait_ge(blk_used[r], f)
                nc.gpsimd.tensor_copy(bnow[:, r:r + 1], tile_of(brow[:, r, :], f)).then_inc(bidx, 1)
                pool.wait_ge(bidx, 2 * f + r + 1)
                alone(pool)
                pool.indirect_dma_start(xblk[r][:, :, :].rearrange("p k f -> p (k f)"), None, edge,
                                        bass.IndirectOffsetOnAxis(ap=bnow[:, r:r + 1], axis=0),
                                        bounds_check=E - K, oob_is_err=False).then_inc(blk_in[r], 16)

            def body(i, units, T, B, E_):
                if units:
                    for q in range(UPI):
                        if q == 2 and T:
                            gather_blocks(1, i - 1)
                        pool.wait_ge(idx_in[q], (i + 1) * 16)
                        if not (isinstance(i, int) and i == 0 and q < 2):
                            u2 = i * UPI + q - 2
                            pool.wait_ge(pair_done, ended(pool, u2 + 1) + (u2 + 1 + DONE0))
                            alone(pool)
                        for j in range(J):
                            pool.indirect_dma_start(rows[q % 2][:, j, :], None, hsplit,
                                                    bass.IndirectOffsetOnAxis(ap=sidx[:, q, j:j + 1], axis=0),
                                                    bounds_check=NPAD - 1, oob_is_err=False
                                                    ).then_inc(rows_in[q % 2], 16)
                    gather_blocks(0, i)
                elif T:
                    gather_blocks(1, i - 1)

            run(pool, body)

            redo = pool.value_load(flags[0:1, 0:1], min_val=0, max_val=1)
            most = pool.value_load(flags[0:1, 1:2], min_val=0, max_val=E)
            with pool.If(redo):
                n = pool.alloc_register("redo_blocks")
                pool.reg_mov(n, 0)
                with pool.Fori(0, NT):
                    with pool.Fori(0, most, K):
                        pool.reg_add(n, n, 1)
                        pool.wait_ge(r_idx, n)
                        alone(pool)
                        pool.indirect_dma_start(xblk[0][:, :, :].rearrange("p k f -> p (k f)"), None, edge,
                                                bass.IndirectOffsetOnAxis(ap=rxu, axis=0),
                                                bounds_check=E - K, oob_is_err=False).then_inc(r_in, 16)

        @block.scalar
        def _(act):
            def copy(o, i, scale=1.0):
                return nc.scalar.activation(o, i, ACT.Copy, scale=scale)

            act.dma_start(u_c[:, :], u0).then_inc(l_c, 16)
            act.dma_start(w1u, w1[D + 3 * F:D + 3 * F + 64, :]).then_inc(l_c, 16)
            act.dma_start(brel_c[:, :], brel).then_inc(l_c, 16)
            act.dma_start(gb[:, :], bih).then_inc(l_c, 16)
            act.dma_start(gb2[:, :], bhh).then_inc(l_c, 16)
            act.dma_start(b1_c[:, :], b1).then_inc(l_c, 16)

            def write_h(g):
                act.wait_ge(ln_split, g + 1)
                act.dma_start(hsplit[g * LNG * P:(g + 1) * LNG * P, :].rearrange("(t p) d -> p t d", p=P),
                              hs[g % 2]).then_inc(h_out[g % 2], 16)

            for g in range(NT // LNG):
                act.wait_ge(ln_stats, g + 1)
                if g >= 2:
                    act.wait_ge(h_out[g % 2], 16 * (g // 2))
                for t in range(LNG):
                    c = g * LNG + t
                    last = nc.scalar.activation(hg[g % 2][:, t, :], xg[g % 2][:, t, :], ACT.Relu,
                                                bias=nm[:, c:c + 1], scale=rs[:, c:c + 1])
                last.then_inc(sc_hg, 1)
                act.wait_ge(sc_hg, g + 1)
                copy(hs[g % 2][:, :, 0:D], hg[g % 2], HSCALE).then_inc(ln_h, 1)
                if g >= 1:
                    write_h(g - 1)
            write_h(NT // LNG - 1)

            act.wait_ge(tab_ready, 1)

            BITES = 4

            def shift_block(n, r, q):
                if q == 0:
                    act.wait_ge(mask_ready, 2 * n + r + 1)
                    act.wait_ge(blk_in[r], 16 * (n + 1))
                    if not (first(n) and r == 0):
                        act.wait_ge(neg_used, 2 * n + r)
                step = -(-K // BITES)
                for k in range(q * step, min(K, (q + 1) * step)):
                    last = nc.scalar.activation(xneg[:, k, :], xblk[r][:, k, :], ACT.Identity,
                                                bias=neg[:, r, k:k + 1])
                if q == BITES - 1:
                    last.then_inc(neg_done, 1)

            def stage_h(n, t, sums):
                act.wait_ge(xa_in, 16 * (n + 1))
                if not first(n):
                    act.wait_ge(te_T, n)
                nc.scalar.activation(xa[:, :], xa[:, :], ACT.Relu, bias=tile_of(nm, t), scale=tile_of(rs, t))
                if sums is not None:
                    act.wait_ge(added, sums)
                copy(aggs[:, :], agg[:, ds(t, 1), :].rearrange("p o d -> p (o d)"), 1.0 / HSCALE).then_inc(sc_h, 1)

            def stage_T(n):
                act.wait_ge(te_T, n + 1)
                if not first(n):
                    act.wait_ge(te_A, n)
                copy(ahT[:, :, :], pTA[:, :, :]).then_inc(sc_T, 1)

            def stage_A(n):
                act.wait_ge(te_A, n + 1)
                if not first(n):
                    act.wait_ge(te_B, 4 * n)
                for m in range(4):
                    last = nc.scalar.activation(h1T[:, m, :], pTA[:, m, :], ACT.Relu, bias=brel_c[:, m:m + 1])
                last.then_inc(sc_A, 1)

            def stage_B(n, m):
                act.wait_ge(te_B, 4 * n + m + 1)
                if m == 0 and not first(n):
                    act.wait_ge(ve_hl, n)
                for g, (row, func) in enumerate(((0, ACT.Sigmoid), (2, ACT.Tanh), (3, ACT.Sigmoid))):
                    last = nc.scalar.activation(gio[:, g, m, :], pB[m % 2][:, g, :], func,
                                                bias=gb[:, 4 * row + m:4 * row + m + 1])
                last.then_inc(sc_B, 1)

            def stage_tc(n):
                act.wait_ge(ve_c, n + 1)
                nc.scalar.activation(gio[:, 0, :, :], gio[:, 1, :, :], ACT.Tanh).then_inc(sc_tc, 1)

            def stage_T3(n):
                act.wait_ge(te_T3, n + 1)
                if not first(n):
                    act.wait_ge(te_D, 2 * n)
                copy(featT[:, :, :], pT23[0:F, 0:3 * P].rearrange("p (c n) -> p c n", c=3)).then_inc(sc_T3, 1)

            def stage_h2(n):
                act.wait_ge(ve_ln, n + 1)
                if not first(n):
                    act.wait_ge(te_T2, n)
                nc.scalar.activation(h2[:, :], x2[:, :], ACT.Relu, bias=nm2[:, :], scale=rs2[:, :]).then_inc(sc_h2, 1)

            def stage_T2(n):
                act.wait_ge(te_T2, n + 1)
                if not first(n):
                    act.wait_ge(te_D, 2 * n)
                copy(h2T[:, :, :], pT2.rearrange("p (k n) -> p k n", k=2)).then_inc(sc_T2, 1)

            def stage_D(n, g):
                act.wait_ge(te_D, 2 * n + g + 1)
                if g == 0 and not first(n):
                    act.wait_ge(te_E, n)
                for m in range(4):
                    last = nc.scalar.activation(zT[:, 4 * g + m, :], pB[g][:, m, :], ACT.Relu,
                                                bias=b1_c[:, 4 * g + m:4 * g + m + 1])
                last.then_inc(sc_D, 1)

            def body(i, units, T, B, E_):
                def second(q):
                    if T:
                        shift_block(i - 1, 1, q)

                def next_first(q):
                    if units:
                        shift_block(i, 0, q)

                if B:
                    stage_B(i - 2, 0)
                    stage_B(i - 2, 1)
                if T:
                    whole = PAIRS + 2 + ADDED0 if not units else ended(act, i * UPI + 1) + (i * UPI + 2 + ADDED0)
                    stage_h(i - 1, i - 1, whole)
                second(0)
                if T:
                    stage_T(i - 1)
                second(1)
                if B:
                    stage_B(i - 2, 2)
                second(2)
                if B:
                    stage_B(i - 2, 3)
                    stage_tc(i - 2)
                    stage_T3(i - 2)
                second(3)
                if B:
                    stage_h2(i - 2)
                if T:
                    stage_A(i - 1)
                if B:
                    stage_T2(i - 2)
                next_first(0)
                next_first(1)
                if B:
                    stage_D(i - 2, 0)
                next_first(2)
                next_first(3)
                if B:
                    stage_D(i - 2, 1)

            run(act, body)

            redo = act.value_load(flags[0:1, 0:1], min_val=0, max_val=1)
            with act.If(redo):
                with act.Fori(0, NT) as t:
                    n = t + NT
                    stage_h(n, t, None)
                    stage_T(n)
                    stage_A(n)
                    for m in range(4):
                        stage_B(n, m)
                    stage_tc(n)
                    stage_T3(n)
                    stage_h2(n)
                    stage_T2(n)
                    stage_D(n, 0)
                    stage_D(n, 1)

        @block.tensor
        def _(pe):
            def mm(o, l, r, a, b):
                return nc.tensor.matmul(o, l, r, start=a, stop=b)

            pe.sem_inc(pair_done, DONE0)
            pe.wait_ge(consts, 11)
            pe.wait_ge(erow_ready, 1)
            pTf = pTA[:, :, :].rearrange("p a n -> p (a n)")
            mm(pTf[:, 0:NB], ones1, erow, True, True).then_inc(ends_ready, 1)
            pe.wait_ge(l_c, 16 * 6)
            for m in range(8):
                last = mm(pT23[:, m:m + 1], w1u[:, m * P:(m + 1) * P], u_c[:, :], True, True)
            last.then_inc(bias_mm, 1)
            pe.wait_ge(start_ready, 1)
            mm(pF[:, 0:NT], shA, start[:, 0:NT], True, False)
            mm(pF[:, 0:NT], shB, start[:, 1:NT + 1], False, True).then_inc(shifted, 1)
            pe.wait_ge(mcnt_ready, 1)
            nc.tensor.transpose(pF[0:1, 256:256 + P], mcnt, ident[:, :]).then_inc(mcnt_T, 1)
            pe.wait_ge(tab_ready, 1)
            pe.wait_ge(l_w, 16 * 11)

            def pairs(u, q, v):
                pe.wait_ge(rows_in[q], 16 * J * (v + 1))
                alone(pe)
                with pe.Fori(ended(pe, u), ended(pe, u + 1) + 1) as t:
                    p = pe.snap(t + u)
                    k = pe.snap(p & (RING - 1))
                    bank = pe.snap(p % BANKS)
                    pe.wait_ge(hot_ready, p + 1)
                    pe.wait_ge(added, p + ADDED0)
                    for j in range(J):
                        for half in range(2):
                            last = mm(acc[:, ds(bank, 1), 0:D], hot[:, ds(k, 1), j, :],
                                      rows[q][:, j, half * D:(half + 1) * D], j + half == 0, j + half == J)
                    last.then_inc(pair_done, 1)

            def stage_T(n):
                pe.wait_ge(sc_h, n + 1)
                if not first(n):
                    pe.wait_ge(sc_A, n)
                for c in range(2):
                    nc.tensor.transpose(pTA[:, c, :], aggs[:, c * P:(c + 1) * P], ident[:, :])
                for c in range(2):
                    last = nc.tensor.transpose(pTA[:, 2 + c, :], xa[:, c * P:(c + 1) * P], ident[:, :])
                last.then_inc(te_T, 1)

            def stage_A(n):
                pe.wait_ge(sc_T, n + 1)
                for m in range(4):
                    for c in range(4):
                        w = (Wrel, Wroot)[c // 2]
                        last = mm(pTA[:, m, :], w[:, c % 2, m * P:(m + 1) * P], ahT[:, c, :], c == 0, c == 3)
                last.then_inc(te_A, 1)

            def stage_B(n, ms):
                pe.wait_ge(sc_A, n + 1)
                for m in ms:
                    if m >= 2:
                        pe.wait_ge(sc_B, 4 * n + m - 1)
                    elif not first(n):
                        pe.wait_ge(sc_D, 2 * n - 1 + m)
                    for g in range(G3):
                        for c in range(4):
                            last = mm(pB[m % 2][:, g, :], Wih[:, c, g, m * P:(m + 1) * P], h1T[:, c, :], c == 0, c == 3)
                    last.then_inc(te_B, 1)

            def stage_FC(n):
                pe.wait_ge(ve_hl, n + 1)
                if not first(n):
                    pe.wait_ge(ve_out, n)
                for c in range(4):
                    last = mm(pFE, hlT[:, c, :], Wfc[:, c, :], c == 0, c == 3)
                last.then_inc(te_FC, 1)

            def stage_T3(n):
                pe.wait_ge(feat_ready, n + 1)
                if not first(n):
                    pe.wait_ge(sc_T2, n)
                for c in range(3):
                    last = nc.tensor.transpose(pT23[0:F, c * P:(c + 1) * P], feat[:, c, :], ident[:, :])
                last.then_inc(te_T3, 1)

            def stage_T2(n):
                pe.wait_ge(sc_h2, n + 1)
                pe.wait_ge(sc_T3, n + 1)
                for c in range(2):
                    last = nc.tensor.transpose(pT2[:, c * P:(c + 1) * P], h2[:, c * P:(c + 1) * P], ident[:, :])
                last.then_inc(te_T2, 1)

            def stage_D(n):
                pe.wait_ge(sc_T3, n + 1)
                for g in range(2):
                    pe.wait_ge(sc_B, 4 * n + 3 + g)
                    for m in range(4):
                        w = slice((4 * g + m) * P, (4 * g + m + 1) * P)
                        for c in range(3):
                            mm(pB[g][:, m, :], W1e[:, c, w], featT[:, c, :], c == 0, False)
                        if g == 0 and m == 0:
                            pe.wait_ge(sc_T2, n + 1)
                        for c in range(2):
                            last = mm(pB[g][:, m, :], W1h[:, c, w], h2T[:, c, :], False, c == 1)
                    last.then_inc(te_D, 1)

            def stage_E(n):
                pe.wait_ge(sc_D, 2 * n + 2)
                pe.wait_ge(ve_x2, n + 1)
                for c in range(8):
                    last = mm(pFE, zT[:, c, :], W2[:, c, :], c == 0, c == 7)
                last.then_inc(te_E, 1)

            def body(i, units, T, B, E_):
                def pairs_of(q):
                    if units:
                        pairs(i * UPI + q, q % 2, 2 * i + q // 2)

                pairs_of(0)
                if B:
                    stage_B(i - 2, (0, 1))
                if E_:
                    stage_E(i - 3)
                pairs_of(1)
                if T:
                    stage_T(i - 1)
                if B:
                    stage_B(i - 2, (2, 3))
                pairs_of(2)
                if B:
                    stage_T3(i - 2)
                    stage_FC(i - 2)
                if T:
                    stage_A(i - 1)
                pairs_of(3)
                if B:
                    stage_T2(i - 2)
                    stage_D(i - 2)

            run(pe, body)

            redo = pe.value_load(flags[0:1, 0:1], min_val=0, max_val=1)
            with pe.If(redo):
                with pe.Fori(0, NT) as t:
                    n = t + NT
                    stage_T(n)
                    stage_A(n)
                    stage_B(n, range(4))
                    stage_FC(n)
                    stage_T3(n)
                    stage_T2(n)
                    stage_D(n)
                    stage_E(n)

        @block.vector
        def _(dve):
            ts, tt, stt = nc.vector.tensor_scalar, nc.vector.tensor_tensor, nc.vector.scalar_tensor_tensor
            copy, reduce = nc.vector.tensor_copy, nc.vector.tensor_reduce

            def chain(sem_, count):
                def link(ins):
                    nonlocal count
                    count = count + 1
                    ins.then_inc(sem_, 1)
                    dve.wait_ge(sem_, count)
                return link

            pro = chain(pd, 0)

            def rstd(link, y, var, v, s):
                link(ts(v, var, EPS, None, ALU.add))
                link(ts(s.bitcast(i32), v.bitcast(i32), 1, None, ALU.logical_shift_right))
                link(ts(y.bitcast(i32), s.bitcast(i32), -1.0, float(0x5F3759DF), ALU.mult, ALU.add))
                link(ts(v, v, -0.5, None, ALU.mult))
                for _ in range(3):
                    if y.shape[1] == 1:
                        link(stt(s, y, v, y, ALU.mult, ALU.mult))
                    else:
                        link(tt(s, y, y, ALU.mult))
                        link(tt(s, s, v, ALU.mult))
                    link(stt(y, s, 1.5, y, ALU.add, ALU.mult))

            dve.wait_ge(l_e, 16)
            copy(erow, erow_i).then_inc(erow_ready, 1)
            dve.wait_ge(ends_ready, 1)
            pro(copy(ends_b, pTA[:, :, :].rearrange("p a n -> p (a n)")[:, 0:NB]))
            dve.wait_ge(consts, 11)
            for g in range(NT // LNG):
                for t in range(g * LNG, (g + 1) * LNG):
                    pro(ts(junk, ends_b, node[:, t:t + 1], 0.0, ALU.is_lt, ALU.add, accum_out=blk[:, t:t + 1]))
                w = slice(g * LNG, (g + 1) * LNG)
                pro(ts(blk[:, w], blk[:, w], float(NB - 1), None, ALU.min))
                copy(blku[:, w], blk[:, w]).then_inc(coarse_ready, LNG)

            for g in range(NT // LNG):
                w = slice(g * LNG, (g + 1) * LNG)
                dve.wait_ge(l_x[g % 2], 16 * (g // 2 + 1))
                for t in range(LNG):
                    last = nc.vector.bn_stats(st[:, t, :], xg[g % 2][:, t, :])
                pro(last)
                for t in range(LNG):
                    last = nc.vector.bn_aggr(mv[:, t, :], st[:, t, :])
                pro(last)
                rstd(pro, rs[:, w], mv[:, :, 1], lna[:, :], lnb[:, :])
                stt(nm[:, w], mv[:, :, 0], -1.0, rs[:, w], ALU.mult, ALU.mult).then_inc(ln_stats, 1)
                for q in range(LNG):
                    t = g * LNG + q
                    dve.wait_ge(fine_in[t % SLOTS], 16 * (t // SLOTS + 1))
                    ts(junk[:, 0:SB], fine[t % SLOTS], node[:, t:t + 1], 0.0, ALU.is_lt, ALU.add,
                       accum_out=start[:, t:t + 1]).then_inc(fine_used, 1)
                    dve.wait_ge(fine_used, t + 1)
                dve.wait_ge(ln_h, g + 1)
                stt(hs[g % 2][:, :, D:2 * D], hg[g % 2], HSCALE, hs[g % 2][:, :, 0:D],
                    ALU.mult, ALU.subtract).then_inc(ln_split, 1)

            nc.vector.memset(start[:, NT:NT + 1], float(E))
            pro(stt(start[:, 0:NT], blk[:, :], float(SB), start[:, 0:NT], ALU.mult, ALU.add))
            start_ready_ins = copy(junk[:, 0:1], start[:, NT:NT + 1])
            start_ready_ins.then_inc(start_ready, 1)
            dve.wait_ge(l_d, 16)
            copy(dtab[:, :], d32)
            dve.wait_ge(l_c, 16 * 6)
            tt(gb[:, :], gb[:, :], gb2[:, :], ALU.add)
            dve.wait_ge(bias_mm, 1)
            tt(b1_c[:, :], b1_c[:, :], pT23[:, 0:8], ALU.add)
            dve.wait_ge(shifted, 1)
            pro(copy(end[:, :], pF[:, 0:NT]))
            pro(tt(cntt, end[:, :], start[:, 0:NT], ALU.subtract))
            reduce(mcnt, cntt, AX.X, ALU.max).then_inc(mcnt_ready, 1)
            ts(hasany[:, :], cntt, 0.0, None, ALU.is_gt)
            pro(ts(rcnt[:, :], cntt, 1.0, None, ALU.max))
            pro(nc.vector.reciprocal(rcnt[:, :], rcnt[:, :]))
            for r in range(NR):
                s, far = cntt, rcnt_tmp
                pro(ts(s, start[:, 0:NT], float(K * r), None, ALU.add))
                pro(ts(browf, s, float(E - K), None, ALU.min))
                pro(tt(blo[:, r, :], s, browf, ALU.subtract))
                pro(tt(bhi[:, r, :], end[:, :], browf, ALU.subtract))
                pro(tt(far, s, end[:, :], ALU.is_ge))
                pro(stt(browf, far, FAR, browf, ALU.mult, ALU.add))
                pro(copy(brow[:, r, :], browf))
            for q in range(2):
                dve.wait_ge(h_out[q], 16 * ((NT // LNG + 1 - q) // 2))
            tile_end = start[0:1, 1:NT + 1]
            pro(tt(cmp, tile_end.unsqueeze(1).to_broadcast([1, NU, NT]), lim.unsqueeze(2).to_broadcast([1, NU, NT]),
                   ALU.is_le))
            nc.vector.memset(tabf[:, 0:1], 0.0)
            pro(reduce(tabf[:, 1:NU + 1], cmp, AX.X, ALU.add))
            pro(copy(tab[:, :], tabf))
            pro(ts(limt, base[0:1, 1:NT + 1], float(UPI * UNIT // P), float(UNIT), ALU.mult, ALU.add))
            pro(tt(cmpt, tile_end, limt, ALU.is_gt))
            dve.wait_ge(mcnt_T, 1)
            pro(reduce(fl[:, 0:1], cmpt, AX.X, ALU.max))
            pro(reduce(fl[:, 1:2], pF[0:1, 256:256 + P], AX.X, ALU.max))
            pro(ts(fl[:, 2:3], fl[:, 1:2], float(NR * K), None, ALU.is_gt))
            pro(tt(fl[:, 0:1], fl[:, 0:1], fl[:, 2:3], ALU.max))
            pro(copy(flags[:, :], fl[:, 0:2]))
            nc.vector.memset(aflat, 0.0).then_inc(added, ADDED0 - 1)
            for b in range(BANKS):
                last = nc.vector.memset(acc[:, b, :], 0.0)
            last.then_inc(added, 1)
            for r in range(NR):
                nc.vector.memset(xblk[r][:, :, :], 0.0)
            pro(nc.vector.memset(xneg[:, :, :], 0.0))

            def masks(n, r):
                link = chain(mchain, (n * NR + r) * 2)
                link(ts(mask[:, r, :], col[:, 0:K], tile_of(blo[:, r, :], n), None, ALU.is_ge))
                link(stt(mask[:, r, :], col[:, 0:K], tile_of(bhi[:, r, :], n), mask[:, r, :], ALU.is_lt, ALU.mult))
                ts(neg[:, r, :], mask[:, r, :], 1.0, BIG, ALU.subtract, ALU.mult).then_inc(mask_ready, 1)

            pro(copy(junk[:, 0:1], xneg[:, 0, 0:1]))
            dve.sem_inc(tab_ready, 1)

            one, two = dve.alloc_register("tile_one_back"), dve.alloc_register("tile_two_back")
            dve.reg_mov(one, NT)
            dve.reg_mov(two, NT)

            def add_sums(p):
                dve.wait_ge(pair_done, p + (DONE0 - 1))
                dve.wait_ge(added, p + ADDED0)
                to = agg[:, ds(dve.snap(two), 1), :]
                tt(to, to, acc[:, ds((p + 1) % BANKS, 1), 0:D], ALU.add).then_inc(added, 1)

            def pairs(u):
                with dve.Fori(ended(dve, u), ended(dve, u + 1) + 1) as t:
                    p = dve.snap(t + u)
                    dve.wait_ge(pair_done, p + 1)
                    stt(hot[:, ds(p & (RING - 1), 1), :, :].rearrange("p o j n -> p (o j) n"),
                        dtab[:, ds(u * J, J)].unsqueeze(2).to_broadcast([P, J, P]), tile_of(base, t),
                        col[:, :].unsqueeze(1).to_broadcast([P, J, P]), ALU.subtract, ALU.is_equal
                        ).then_inc(hot_ready, 1)
                    add_sums(p)
                    dve.reg_mov(two, one)
                    dve.reg_mov(one, t)

            def block_max(n, r):
                dve.wait_ge(neg_done, 2 * n + r + 1)
                reduce(part[:, r, 1, :], xneg[:, :, :].rearrange("p k f -> p f k"), AX.X, ALU.max).then_inc(neg_used, 1)

            def block_own(n, r):
                chain(fchain, n * NR + r)(
                    tt(xblk[r][:, :, :], xblk[r][:, :, :], mask[:, r, :].unsqueeze(2).to_broadcast([P, K, F]), ALU.mult))

            def block_sum(n, r):
                reduce(part[:, r, 0, :], xblk[r][:, :, :].rearrange("p k f -> p f k"), AX.X, ALU.add).then_inc(blk_used[r], 1)

            def features(link, n, t, s, m):
                if not first(n):
                    dve.wait_ge(te_T3, n)
                link(ts(feat[:, 1, :], m, tile_of(hasany, t), None, ALU.mult))
                copy(feat[:, 0, :], s)
                ts(feat[:, 2, :], s, tile_of(rcnt, t), None, ALU.mult).then_inc(feat_ready, 1)

            def combine(n, t):
                link = chain(rchain, n * 3)
                link(tt(part[:, 0, 1, :], part[:, 0, 1, :], part[:, 1, 1, :], ALU.max))
                link(tt(part[:, 0, 0, :], part[:, 0, 0, :], part[:, 1, 0, :], ALU.add))
                features(link, n, t, part[:, 0, 0, :], part[:, 0, 1, :])

            def stage_c(n):
                dve.wait_ge(sc_B, 4 * n + 4)
                tt(gio[:, 1, :, :], gio[:, 0, :, :], gio[:, 1, :, :], ALU.mult).then_inc(ve_c, 1)
                dve.wait_ge(sc_tc, n + 1)
                if not first(n):
                    dve.wait_ge(te_FC, n)
                tt(hlT[:, :, :], gio[:, 0, :, :], gio[:, 2, :, :], ALU.mult).then_inc(ve_hl, 1)

            def stage_LN(n):
                link = chain(lchain, n * 14)
                dve.wait_ge(te_FC, n + 1)
                dve.wait_ge(xf_in, 16 * (n + 1))
                tt(x2[:, :], pFE, xf[:, :], ALU.add).then_inc(ve_x2, 1)
                dve.wait_ge(ve_x2, n + 1)
                link(tt(x2[:, :], x2[:, :], bfc_r[:, :], ALU.add))
                link(nc.vector.bn_stats(st[:, 0, :], x2[:, :]))
                alone(dve)
                link(nc.vector.bn_aggr(mv[:, 0, :], st[:, 0, :]))
                rstd(link, rs2[:, :], mv[:, 0, 1:2], lna[:, 0:1], lnb[:, 0:1])
                link(stt(nm2[:, :], mv[:, 0, 0:1], -1.0, rs2[:, :], ALU.mult, ALU.mult))
                dve.sem_inc(ve_ln, 1)

            def stage_res(n):
                link = chain(schain, n)
                dve.wait_ge(sc_h2, n + 1)
                link(tt(x2[:, :], x2[:, :], h2[:, :], ALU.add))
                tt(x2[:, :], x2[:, :], b2_r[:, :], ALU.add).then_inc(ve_res, 1)

            def stage_out(n):
                dve.wait_ge(te_E, n + 1)
                dve.wait_ge(ve_res, n + 1)
                if not first(n):
                    dve.wait_ge(stored, 16 * n)
                tt(ob[:, :], pFE, x2[:, :], ALU.add).then_inc(ve_out, 1)

            def body(i, units, T, B, E_):
                whole_loop = not (isinstance(i, int) and i == NT - 1)

                def pairs_ahead(q):
                    if units and (q < UPI or whole_loop):
                        pairs(i * UPI + q)
                    elif units:
                        add_sums(PAIRS)
                        dve.reg_mov(two, one)
                        add_sums(PAIRS + 1)

                pairs_ahead(1)
                if T:
                    block_max(i - 1, 0)
                    block_own(i - 1, 0)
                    block_sum(i - 1, 0)
                pairs_ahead(2)
                if E_:
                    stage_out(i - 3)
                if B:
                    stage_c(i - 2)
                pairs_ahead(3)
                if B:
                    stage_LN(i - 2)
                if T:
                    block_max(i - 1, 1)
                    block_own(i - 1, 1)
                if units:
                    masks(i, 0)
                pairs_ahead(4)
                if T:
                    block_sum(i - 1, 1)
                    combine(i - 1, i - 1)
                if B:
                    stage_res(i - 2)
                if units:
                    masks(i, 1)

            pairs(0)
            run(dve, body)

            redo = dve.value_load(flags[0:1, 0:1], min_val=0, max_val=1)
            most = dve.value_load(flags[0:1, 1:2], min_val=0, max_val=E)
            with dve.If(redo):
                n_link, n_blk = dve.alloc_register("redo_links"), dve.alloc_register("redo_blocks_v")
                dve.reg_mov(n_link, 0)
                dve.reg_mov(n_blk, 0)

                def link(ins):
                    ins.then_inc(rdchain, 1)
                    dve.reg_add(n_link, n_link, 1)
                    dve.wait_ge(rdchain, n_link)

                s, m = part[:, 0, 0, :], part[:, 0, 1, :]
                own, off = neg[:, 0, :], neg[:, 1, :]
                row, lo, hi, far = (rx[:, q:q + 1] for q in range(4))
                nxt = rx[:, 4:5]
                with dve.Fori(0, NT) as t:
                    link(nc.vector.memset(s, 0.0))
                    link(nc.vector.memset(m, -BIG))
                    link(copy(nxt, tile_of(start, t)))
                    alone(dve)
                    with dve.Fori(0, most, K):
                        link(ts(row, nxt, float(E - K), None, ALU.min))
                        link(tt(lo, nxt, row, ALU.subtract))
                        link(tt(hi, tile_of(end, t), row, ALU.subtract))
                        link(tt(far, nxt, tile_of(end, t), ALU.is_ge))
                        link(stt(row, far, FAR, row, ALU.mult, ALU.add))
                        link(copy(rxu, row))
                        dve.sem_inc(r_idx, 1)
                        link(ts(nxt, nxt, float(K), None, ALU.add))
                        link(ts(own, col[:, 0:K], lo, None, ALU.is_ge))
                        link(stt(own, col[:, 0:K], hi, own, ALU.is_lt, ALU.mult))
                        link(ts(off, own, 1.0, BIG, ALU.subtract, ALU.mult))
                        dve.reg_add(n_blk, n_blk, 16)
                        dve.wait_ge(r_in, n_blk)
                        blk_ = xblk[0][:, :, :]
                        link(tt(xneg[:, :, :], blk_, own.unsqueeze(2).to_broadcast([P, K, F]), ALU.mult))
                        link(reduce(part[:, 1, 0, :], xneg[:, :, :].rearrange("p k f -> p f k"), AX.X, ALU.add))
                        link(tt(s, s, part[:, 1, 0, :], ALU.add))
                        link(tt(xneg[:, :, :], blk_, off.unsqueeze(2).to_broadcast([P, K, F]), ALU.add))
                        link(reduce(part[:, 1, 1, :], xneg[:, :, :].rearrange("p k f -> p f k"), AX.X, ALU.max))
                        link(tt(m, m, part[:, 1, 1, :], ALU.max))
                        alone(dve)
                    n = t + NT
                    features(link, n, t, s, m)
                    stage_c(n)
                    stage_LN(n)
                    stage_res(n)
                    stage_out(n)


def kernel(**inputs):
    import numpy as np
    import concourse.bacc as bacc
    from concourse.bass_utils import run_bass_kernel_spmd

    a = {k: np.asarray(v) for k, v in inputs.items()}

    def padded(v, n, fill):
        o = np.full((n,) + v.shape[1:], fill, v.dtype)
        o[:v.shape[0]] = v
        return o

    def by_partition(v):
        return np.ascontiguousarray(v.reshape(-1, P).T)

    arrays = {
        "x": padded(a["x"], NPAD, 0),
        "src": padded(a["src"], EPAD, 0).reshape(EPAD, 1),
        "dst": padded(a["dst"], EPAD, NPAD + P),
        "edge": np.ascontiguousarray(a["edge_attr_96"]),
        "wrel": np.ascontiguousarray(a["L0_gnn_W_rel"]),
        "brel": by_partition(a["L0_gnn_b_rel"]),
        "wroot": np.ascontiguousarray(a["L0_gnn_W_root"]),
        "wih": np.ascontiguousarray(a["L0_gnn_W_ih"].T),
        "bih": by_partition(a["L0_gnn_b_ih"]),
        "bhh": by_partition(a["L0_gnn_b_hh"]),
        "wfc": np.ascontiguousarray(a["L0_gnn_W_fc"]),
        "bfc": a["L0_gnn_b_fc"].reshape(1, D),
        "u0": np.ascontiguousarray(a["L1_gnn_u"][0].reshape(-1, 1)),
        "w1": np.ascontiguousarray(a["L1_gnn_W1"]),
        "b1": by_partition(a["L1_gnn_b1"]),
        "w2": np.ascontiguousarray(a["L1_gnn_W2"]),
        "b2": a["L1_gnn_b2"].reshape(1, D),
    }
    nc = bacc.Bacc("TRN2", target_bir_lowering=False, num_devices=1, dynamic_dma_scratch_size=8192)
    args = [nc.dram_tensor(f"in_{k}", v.shape, mybir.dt.uint32 if k == "src" else mybir.dt.from_np(v.dtype),
                           kind="ExternalInput").ap() for k, v in arrays.items()]
    out = nc.dram_tensor("out", (NPAD, D), mybir.dt.float32, kind="ExternalOutput").ap()
    build(nc, *args, out)
    r = run_bass_kernel_spmd(nc, [{f"in_{k}": v.view(np.uint32) if k == "src" else v for k, v in arrays.items()}],
                             core_ids=[0])
    return r.results[0]["out"][:N]
```

```python
import concourse.bass as bass
from concourse import mybir
from contextlib import ExitStack

N, E = 6250, 200000
D, F, H, G3, Z = 256, 96, 512, 3, 1024
P = 128
NT = -(-N // P)
NPAD = NT * P
J = 8
UNIT = P * J
NU = -(-E // UNIT)
UPI = 4
EPAD = NU * UNIT
K = 30
NR = 2
SB = 400
NB = E // SB
LNG = 7
RING = 4
BANKS = 3
HSCALE = 1024.0
BIG = 3.0e38
EPS = 1e-5
FAR = 10000000.0
PAIRS = NU + NT
assert NU == UPI * NT and NT % LNG == 0 and E % SB == 0


def build(nc, x, src, dst, edge, wrel, brel, wroot, wih, bih, bhh, wfc, bfc, u0, w1, b1, w2, b2, out):
    f32, f16, i32, i16, u32 = (mybir.dt.float32, mybir.dt.float16, mybir.dt.int32, mybir.dt.int16,
                               mybir.dt.uint32)
    ALU, ACT, AX = mybir.AluOpType, mybir.ActivationFunctionType, mybir.AxisListType
    ds = bass.ds

    hsplit = nc.dram_tensor("hsplit", (NPAD, 2 * D), f16).ap()

    with ExitStack() as ctx:
        def sb(name, shape, dt):
            return ctx.enter_context(nc.sbuf_tensor(name, shape, dt))

        def pb(name, shape, dt):
            return ctx.enter_context(nc.psum_tensor(name, shape, dt))

        def sem(name):
            return ctx.enter_context(nc.semaphore(name))

        Wrel = sb("Wrel", [P, 2, H], f32)
        Wroot = sb("Wroot", [P, 2, H], f32)
        Wih = sb("Wih", [P, 4, G3, H], f32)
        Wfc = sb("Wfc", [P, 4, D], f32)
        W1h = sb("W1h", [P, 2, Z], f32)
        W1e = sb("W1e", [F, 3, Z], f32)
        W2 = sb("W2", [P, 8, D], f32)
        brel_c = sb("brel_c", [P, 4], f32)
        gb = sb("gb", [P, 16], f32)
        gb2 = sb("gb2", [P, 16], f32)
        b1_c = sb("b1_c", [P, 8], f32)
        bfc_r = sb("bfc_r", [P, D], f32)
        b2_r = sb("b2_r", [P, D], f32)
        u_c = sb("u_c", [64, 1], f32)
        ident = sb("ident", [P, P], f32)
        node = sb("node", [P, NT], f32)
        base = sb("base", [P, NT + 1], f32)
        col = sb("col", [P, P], f32)
        dtab = sb("dtab", [P, NU * J], i16)
        sidx = sb("sidx", [P, UPI, J], u32)
        start = sb("start", [P, NT + 1], f32)
        end = sb("end", [P, NT], f32)
        hasany = sb("hasany", [P, NT], f32)
        rcnt = sb("rcnt", [P, NT], f32)
        blk = sb("blk", [P, NT], f32)
        blku = sb("blku", [P, NT], u32)
        blo = sb("blo", [P, NR, NT], f32)
        bhi = sb("bhi", [P, NR, NT], f32)
        brow = sb("brow", [P, NR, NT], u32)
        bnow = sb("bnow", [P, NR], u32)
        tab = sb("tab", [1, NU + 2], i32)
        flags = sb("flags", [1, 2], i32)
        agg = sb("agg", [P, NT + 1, D], f32)
        rows = [sb(f"rows{q}", [P, J, 2 * D], f16) for q in range(2)]
        hot = sb("hot", [P, RING, P, J], f16)
        col8 = sb("col8", [P, P, J], f16)
        drel = sb("drel", [P, RING, J], f16)
        xblk = [sb(f"xblk{r}", [P, K, F], f32) for r in range(NR)]
        xneg = sb("xneg", [P, K, F], f32)
        mask = sb("mask", [P, NR, K], f32)
        neg = sb("neg", [P, NR, K], f32)
        part = sb("part", [P, 2, 2, F], f32)
        feat = sb("feat", [P, 3, F], f32)
        xa = sb("xa", [P, D], f32)
        aggs = sb("aggs", [P, D], f32)
        ahT = sb("ahT", [P, 4, P], f32)
        h1T = sb("h1T", [P, 4, P], f32)
        gio = sb("gio", [P, G3, 4, P], f32)
        hlT = sb("hlT", [P, 4, P], f32)
        xf = sb("xf", [P, D], f32)
        x2 = sb("x2", [P, D], f32)
        h2 = sb("h2", [P, D], f32)
        h2T = sb("h2T", [P, 2, P], f32)
        featT = sb("featT", [F, 3, P], f32)
        zT = sb("zT", [P, 8, P], f32)
        ob = sb("ob", [P, D], f32)
        rs = sb("rs", [P, NT], f32)
        nm = sb("nm", [P, NT], f32)
        st = sb("st", [P, LNG, 6], f32)
        mv = sb("mv", [P, LNG, 2], f32)
        lna = sb("lna", [P, LNG], f32)
        lnb = sb("lnb", [P, LNG], f32)
        lny = sb("lny", [P, LNG], f32)
        rs2 = sb("rs2", [P, 1], f32)
        nm2 = sb("nm2", [P, 1], f32)
        aflat = agg[:, :, :].rearrange("p t d -> p (t d)")
        GX = LNG * D

        def group(buf, at, dt):
            return buf[:, at:at + GX].bitcast(dt).rearrange("p (t d) -> p t d", t=LNG)

        wihf = Wih[:, :, :, :].rearrange("p k g m -> p (k g m)")
        rows1f = rows[1][:, :, :].rearrange("p j n -> p (j n)").bitcast(f32)
        xg = [group(wihf, 0, f32), group(wihf, GX, f32)]
        hg = [group(wihf, 2 * GX, f32), group(W1h[:, :, :].rearrange("p k m -> p (k m)"), 0, f32)]
        hs = [group(W2[:, :, :].rearrange("p k m -> p (k m)"), 0, f16), group(rows1f, 0, f16)]
        rs_s, nm_s = rcnt, hasany
        SLOTS = 7
        x0f = xblk[0][:, :, :].rearrange("p k f -> p (k f)")
        fine = [x0f[:, q * SB:(q + 1) * SB].bitcast(i32) for q in range(SLOTS)]
        x1f = xblk[1][:, :, :].rearrange("p k f -> p (k f)")
        ends_b = x1f[:, 0:NB // 2].bitcast(i16)
        giof = gio[:, :, :, :].rearrange("p g m n -> p (g m n)")
        zTf = zT[:, :, :].rearrange("p m n -> p (m n)")
        junk = [giof[:, q * SB:(q + 1) * SB] for q in range(3)] + [zTf[:, q * SB:(q + 1) * SB] for q in range(2)] + [
            w[:, :, :].rearrange("p m n -> p (m n)")[:, 0:SB] for w in (ahT, h1T)]
        hotf = [hot[:, q, :, :].rearrange("p n j -> p (n j)").bitcast(f32) for q in range(RING)]
        erow = hotf[2][0:1, 0:NB]
        erow_i = hotf[3][0:1, 0:NB].bitcast(i32)
        d32 = xneg[:, :, :].rearrange("p k f -> p (k f)")[:, 0:NU * J].bitcast(i32)
        xneg_row = xneg[:, :, :].rearrange("p k f -> p (k f)")
        lim = xneg_row[:, 1600:1602]
        tcnt = xneg_row[:, 1610:1612]
        limt = xneg_row[0:1, 1800:1800 + NT]
        cmpt = xneg_row[0:1, 1900:1900 + NT]
        fl = xneg_row[0:1, 2500:2506]
        cntt = xneg_row[:, 2600:2600 + NT]
        mcnt = xneg_row[:, 2700:2701]
        browf = xneg_row[:, 2720:2720 + NT]
        rcnt_tmp = xneg_row[:, 2780:2780 + NT]
        shA, shB = hotf[0][:, 0:P], hotf[1][:, 0:P]
        ones1 = hotf[0][0:1, P:2 * P]
        w1u = rows[0][0:64, :, :].rearrange("p j n -> p (j n)").bitcast(f32)[:, 0:Z]
        rx = mask[:, 0, 0:8]
        rxu = mask[:, 1, 0:1].bitcast(u32)

        acc = pb("acc", [P, BANKS, 512], f32)
        pTA = pb("pTA", [P, 4, P], f32)
        pT23 = pb("pT23", [P, 512], f32)
        pF = pb("pF", [P, 512], f32)
        pB = [pb(f"pB{q}", [P, 4, P], f32) for q in range(2)]
        pFE, pT2 = pF[:, 0:D], pT23[:, 0:D]

        l_wa = sem("l_wa")
        l_w, l_x, l_d, l_e, l_c = sem("l_w"), [sem("l_x0"), sem("l_x1")], sem("l_d"), sem("l_e"), sem("l_c")
        consts = sem("consts")
        pd = sem("pd")
        erow_ready, ends_ready = sem("erow_ready"), sem("ends_ready")
        coarse_ready = sem("coarse_ready")
        fine_in = [sem(f"fine_in{q}") for q in range(SLOTS)]
        fine_used = sem("fine_used")
        start_ready, shifted, bias_mm = sem("start_ready"), sem("shifted"), sem("bias_mm")
        zeroed, tile_ends, tcnt_ready, tcnt_T = sem("zeroed"), sem("tile_ends"), sem("tcnt_ready"), sem("tcnt_T")
        mcnt_ready, mcnt_T = sem("mcnt_ready"), sem("mcnt_T")
        ln_stats, ln_h, ln_split = sem("ln_stats"), sem("ln_h"), sem("ln_split")
        h_out = [sem("h_out0"), sem("h_out1")]
        tab_ready = sem("tab_ready")
        idx_in = [sem(f"idx_in{q}") for q in range(UPI)]
        rows_in = [sem("rows_in0"), sem("rows_in1")]
        drel_ready, hot_ready, pair_done, added = sem("drel_ready"), sem("hot_ready"), sem("pair_done"), sem("added")
        bidx = sem("bidx")
        blk_in = [sem("blk_in0"), sem("blk_in1")]
        blk_used = [sem("blk_used0"), sem("blk_used1")]
        mask_ready, neg_done, own_done = sem("mask_ready"), sem("neg_done"), sem("own_done")
        neg_used, feat_ready = sem("neg_used"), sem("feat_ready")
        fchain = sem("fchain")
        mchain = sem("mchain")
        xa_in, xf_in, stored = sem("xa_in"), sem("xf_in"), sem("stored")
        sc_hg = sem("sc_hg")
        sc_h, te_T, sc_T, te_A, sc_A = sem("sc_h"), sem("te_T"), sem("sc_T"), sem("te_A"), sem("sc_A")
        te_B, sc_B, ve_c, sc_tc, ve_hl = sem("te_B"), sem("sc_B"), sem("ve_c"), sem("sc_tc"), sem("ve_hl")
        te_FC, ve_x2, ve_ln, sc_h2, te_T2, sc_T2 = (sem("te_FC"), sem("ve_x2"), sem("ve_ln"), sem("sc_h2"),
                                                    sem("te_T2"), sem("sc_T2"))
        te_T3, sc_T3, te_D, sc_D, te_E, ve_res, ve_out = (sem("te_T3"), sem("sc_T3"), sem("te_D"), sem("sc_D"),
                                                          sem("te_E"), sem("ve_res"), sem("ve_out"))
        lchain, rchain, schain = sem("lchain"), sem("rchain"), sem("schain")
        r_idx, r_clear, r_in, rdchain = sem("r_idx"), sem("r_clear"), sem("r_in"), sem("rdchain")

        block = ctx.enter_context(nc.Block())

        ADDED0 = 2
        DONE0 = RING

        turn = sem("turn")

        def alone(eng):
            eng.sem_inc(turn, 1)

        def first(n):
            return isinstance(n, int) and n == 0

        def tile_of(ap, t):
            return ap[:, ds(t, 1)]

        def ended(eng, u):
            return eng.value_load(tab[0:1, ds(u, 1)], min_val=0, max_val=NT)

        def unit_tiles(eng):
            lo, hi = eng.alloc_register("first_tile"), eng.alloc_register("last_tile")
            eng.reg_mov(lo, 0)
            eng.reg_mov(hi, ended(eng, 1))

            def step(u):
                eng.reg_mov(lo, hi)
                eng.reg_mov(hi, ended(eng, u + 2))
            return lo, hi, step

        def schedule(body):
            body(0, True, False, False, False)
            body(1, True, True, False, False)
            body(2, True, True, True, False)
            yield
            body(NT - 1, True, True, True, True)
            body(NT, False, True, True, True)
            body(NT + 1, False, False, True, True)
            body(NT + 2, False, False, False, True)

        def run(eng, body):
            steps = schedule(body)
            next(steps)
            with eng.Fori(3, NT - 1) as i:
                body(i, True, True, True, True)
            for _ in steps:
                pass

        @block.sync
        def _(sp):
            sp.dma_start(erow_i, dst[0:E].rearrange("(b s) -> s b", s=SB)[SB - 1:SB, :],
                         allow_slow_non_contiguous=True).then_inc(l_e, 16)
            for g in range(2):
                sp.dma_start(xg[g], x[g * LNG * P:(g + 1) * LNG * P, :].rearrange("(t p) d -> p t d", p=P)).then_inc(l_x[g], 16)
            sp.dma_start(d32.rearrange("p (u j) -> p u j", j=J), dst.rearrange("(u p j) -> p u j", p=P, j=J)).then_inc(l_d, 16)
            for q in range(UPI):
                sp.dma_start(sidx[:, q, :], src[q * UNIT:(q + 1) * UNIT, :].rearrange("(p j) o -> p (j o)", j=J)).then_inc(idx_in[q], 16)
            for g in range(2, NT // LNG):
                sp.wait_ge(sc_hg, g - 1)
                sp.dma_start(xg[g % 2], x[g * LNG * P:(g + 1) * LNG * P, :].rearrange("(t p) d -> p t d", p=P)).then_inc(l_x[g % 2], 16)
            sp.dma_start(xa[:, :], x[0:P, :]).then_inc(xa_in, 16)
            sp.dma_start(xf[:, :], x[0:P, :]).then_inc(xf_in, 16)
            def load(dst_ap, src_ap, signal=l_w):
                sp.dma_start(dst_ap, src_ap).then_inc(signal, 16)

            load(Wrel[:, :, :], wrel.rearrange("(k p) m -> p k m", p=P), l_wa)
            load(Wroot[:, :, :], wroot.rearrange("(k p) m -> p k m", p=P), l_wa)
            sp.wait_ge(ln_split, NT // LNG)
            sp.wait_ge(h_out[0], 16 * ((NT // LNG + 1) // 2))

            def other_weights(i, q):
                if (i, q) in ((0, 1), (0, 2), (0, 3)):
                    g, row = q - 1, (0, 2, 3)[q - 1]
                    load(Wih[:, :, g, :], wih[:, row * H:(row + 1) * H].rearrange("(k p) m -> p k m", p=P))
                elif (i, q) == (1, 0):
                    load(Wfc[:, :, :], wfc.rearrange("(k p) m -> p k m", p=P))
                    load(bfc_r[:, :], bfc.to_broadcast([P, D]))
                    load(b2_r[:, :], b2.to_broadcast([P, D]))
                elif (i, q) == (1, 1):
                    load(W1e[:, :, :], w1[D:D + 3 * F, :].rearrange("(k p) m -> p k m", p=F))
                elif (i, q) == (1, 2):
                    load(W1h[:, :, :], w1[0:D, :].rearrange("(k p) m -> p k m", p=P))
                elif (i, q) == (1, 3):
                    load(W2[:, :, :], w2.rearrange("(k p) m -> p k m", p=P))

            def body(i, units, T, B, E_):
                def next_sources(q):
                    if units and not (isinstance(i, int) and i == NT - 1):
                        sp.wait_ge(rows_in[q % 2], 16 * J * (2 * i + q // 2 + 1))
                        sp.dma_start(sidx[:, q, :], src[ds((i * UPI + UPI + q) * UNIT, UNIT), :]
                                     .rearrange("(p j) o -> p (j o)", j=J)).then_inc(idx_in[q], 16)
                    if isinstance(i, int):
                        other_weights(i, q)

                next_sources(0)
                if E_:
                    sp.wait_ge(ve_out, i - 2)
                    sp.dma_start(out[ds((i - 3) * P, P), :], ob[:, :]).then_inc(stored, 16)
                next_sources(1)
                if T and not (isinstance(i, int) and i == NT):
                    sp.wait_ge(te_T, i)
                    sp.dma_start(xa[:, :], x[ds(i * P, P), :]).then_inc(xa_in, 16)
                next_sources(2)
                next_sources(3)
                if B and not (isinstance(i, int) and i == NT + 1):
                    sp.wait_ge(ve_x2, i - 1)
                    sp.dma_start(xf[:, :], x[ds((i - 1) * P, P), :]).then_inc(xf_in, 16)

            run(sp, body)

            redo = sp.value_load(flags[0:1, 0:1], min_val=0, max_val=1)
            sp.wait_ge(stored, 16 * NT)
            with sp.If(redo):
                with sp.Fori(0, NT) as t:
                    sp.wait_ge(te_T, t + NT)
                    sp.wait_ge(ve_out, t + NT)
                    sp.dma_start(xa[:, :], x[ds(t * P, P), :]).then_inc(xa_in, 16)
                    sp.dma_start(xf[:, :], x[ds(t * P, P), :]).then_inc(xf_in, 16)
                    sp.wait_ge(ve_out, t + NT + 1)
                    sp.dma_start(out[ds(t * P, P), :], ob[:, :]).then_inc(stored, 16)
                    sp.wait_ge(stored, (t + NT + 1) * 16)
                    alone(sp)

        @block.gpsimd
        def _(pool):
            def const(ins):
                ins.then_inc(consts, 1)

            const(nc.gpsimd.iota(node[:, :], [[P, NT]], 0, 1, allow_small_or_imprecise_dtypes=True))
            const(nc.gpsimd.iota(base[:, :], [[P, NT + 1]], 0, 0, allow_small_or_imprecise_dtypes=True))
            const(nc.gpsimd.iota(col[:, :], [[1, P]], 0, 0, allow_small_or_imprecise_dtypes=True))
            const(nc.gpsimd.memset(ident[:, :], 0.0))
            const(nc.gpsimd.memset(shA, 0.0))
            const(nc.gpsimd.memset(shB, 0.0))
            const(nc.gpsimd.memset(ones1, 1.0))
            const(nc.gpsimd.iota(lim, [[UNIT, 2]], UNIT, 2 * UNIT, allow_small_or_imprecise_dtypes=True))
            pool.wait_ge(consts, 8)
            for ap, off in ((ident[:, :], 0), (shA, -1), (shB, P - 1)):
                const(nc.gpsimd.affine_select(out=ap, in_=ap, compare_op=ALU.not_equal, fill=1.0, base=off,
                                              pattern=[[-1, P]], channel_multiplier=1))
            nc.gpsimd.iota(col8[:, :, :], [[1, P], [0, J]], 0, 0, allow_small_or_imprecise_dtypes=True)
            nc.gpsimd.memset(x0f[:, SLOTS * SB:K * F], 0.0)
            nc.gpsimd.memset(x1f[:, NB // 2:K * F], 0.0).then_inc(zeroed, 1)

            drows = dst[0:E].rearrange("(b s) -> b s", s=SB)
            for t in range(NT):
                pool.wait_ge(coarse_ready, t + 1)
                if t >= SLOTS:
                    pool.wait_ge(fine_used, t - SLOTS + 1)
                pool.indirect_dma_start(fine[t % SLOTS], None, drows,
                                        bass.IndirectOffsetOnAxis(ap=blku[:, t:t + 1], axis=0),
                                        bounds_check=NB - 1, oob_is_err=False).then_inc(fine_in[t % SLOTS], 16)
                if t % LNG == LNG - 1:
                    g = t // LNG
                    pool.wait_ge(ln_h, g + 1)
                    nc.gpsimd.tensor_tensor(hs[g % 2][:, :, D:2 * D], hg[g % 2], hs[g % 2][:, :, 0:D],
                                            ALU.subtract).then_inc(ln_split, 1)

            pool.wait_ge(bias_mm, 1)
            for q in range(2):
                pool.wait_ge(h_out[q], 16 * ((NT // LNG + 1 - q) // 2))

            def gather_blocks(r, f):
                if not first(f):
                    pool.wait_ge(blk_used[r], f)
                nc.gpsimd.tensor_copy(bnow[:, r:r + 1], tile_of(brow[:, r, :], f)).then_inc(bidx, 1)
                pool.wait_ge(bidx, 2 * f + r + 1)
                alone(pool)
                pool.indirect_dma_start(xblk[r][:, :, :].rearrange("p k f -> p (k f)"), None, edge,
                                        bass.IndirectOffsetOnAxis(ap=bnow[:, r:r + 1], axis=0),
                                        bounds_check=E - K, oob_is_err=False).then_inc(blk_in[r], 16)

            def body(i, units, T, B, E_):
                if units:
                    for q in range(UPI):
                        if q == 2 and T:
                            gather_blocks(1, i - 1)
                        if isinstance(i, int) and i == 0 and q == 2:
                            pool.wait_ge(tab_ready, 1)
                        pool.wait_ge(idx_in[q], (i + 1) * 16)
                        if not (isinstance(i, int) and i == 0 and q < 2):
                            u2 = i * UPI + q - 2
                            pool.wait_ge(pair_done, ended(pool, u2 + 1) + (u2 + 1 + DONE0))
                            alone(pool)
                        for j in range(J):
                            pool.indirect_dma_start(rows[q % 2][:, j, :], None, hsplit,
                                                    bass.IndirectOffsetOnAxis(ap=sidx[:, q, j:j + 1], axis=0),
                                                    bounds_check=NPAD - 1, oob_is_err=False
                                                    ).then_inc(rows_in[q % 2], 16)
                    gather_blocks(0, i)
                elif T:
                    gather_blocks(1, i - 1)

            run(pool, body)

            redo = pool.value_load(flags[0:1, 0:1], min_val=0, max_val=1)
            most = pool.value_load(flags[0:1, 1:2], min_val=0, max_val=E)
            with pool.If(redo):
                n = pool.alloc_register("redo_blocks")
                pool.reg_mov(n, 0)
                pool.wait_ge(blk_used[0], NT)
                pool.indirect_dma_start(xblk[0][:, :, :].rearrange("p k f -> p (k f)"), None, edge,
                                        bass.IndirectOffsetOnAxis(ap=bnow[:, 0:1], axis=0),
                                        bounds_check=E - K, oob_is_err=False).then_inc(r_in, 16)
                pool.wait_ge(r_in, 16)
                alone(pool)
                with pool.Fori(0, NT):
                    with pool.Fori(0, most, K):
                        pool.reg_add(n, n, 1)
                        pool.wait_ge(r_idx, n)
                        alone(pool)
                        nc.gpsimd.inc_swdge_sem([r_in], [16], mode="sub").then_inc(r_clear, 1)
                        pool.indirect_dma_start(xblk[0][:, :, :].rearrange("p k f -> p (k f)"), None, edge,
                                                bass.IndirectOffsetOnAxis(ap=rxu, axis=0),
                                                bounds_check=E - K, oob_is_err=False).then_inc(r_in, 16)

        @block.scalar
        def _(act):
            def copy(o, i, scale=1.0):
                return nc.scalar.activation(o, i, ACT.Copy, scale=scale)

            act.dma_start(u_c[:, :], u0).then_inc(l_c, 16)
            act.dma_start(w1u, w1[D + 3 * F:D + 3 * F + 64, :]).then_inc(l_c, 16)
            act.dma_start(brel_c[:, :], brel).then_inc(l_c, 16)
            act.dma_start(gb[:, :], bih).then_inc(l_c, 16)
            act.dma_start(gb2[:, :], bhh).then_inc(l_c, 16)
            act.dma_start(b1_c[:, :], b1).then_inc(l_c, 16)

            act.wait_ge(consts, 11)
            len_agg = (NT + 1) * D
            ZPART = -(-len_agg // (NT // LNG))

            def write_h(g):
                act.wait_ge(ln_split, g + 1)
                act.dma_start(hsplit[g * LNG * P:(g + 1) * LNG * P, :].rearrange("(t p) d -> p t d", p=P),
                              hs[g % 2]).then_inc(h_out[g % 2], 16)

            for g in range(NT // LNG):
                act.wait_ge(ln_stats, g + 1)
                if g >= 2:
                    act.wait_ge(h_out[g % 2], 16 * (g // 2))
                for t in range(LNG):
                    c = g * LNG + t
                    last = nc.scalar.activation(hg[g % 2][:, t, :], xg[g % 2][:, t, :], ACT.Relu,
                                                bias=nm_s[:, c:c + 1], scale=rs_s[:, c:c + 1])
                last.then_inc(sc_hg, 1)
                act.wait_ge(sc_hg, g + 1)
                copy(hs[g % 2][:, :, 0:D], hg[g % 2]).then_inc(ln_h, 1)
                last = copy(aflat[:, g * ZPART:min(len_agg, (g + 1) * ZPART)],
                            col[:, 0:1].to_broadcast([P, min(len_agg, (g + 1) * ZPART) - g * ZPART]))
                if g >= 1:
                    write_h(g - 1)
            last.then_inc(added, ADDED0 - 1)
            write_h(NT // LNG - 1)

            act.wait_ge(tab_ready, 1)

            BITES = 4

            def shift_block(n, r, q):
                if q == 0:
                    act.wait_ge(mask_ready, 2 * n + r + 1)
                    act.wait_ge(blk_in[r], 16 * (n + 1))
                    if not (first(n) and r == 0):
                        act.wait_ge(neg_used, 2 * n + r)
                step = -(-K // BITES)
                for k in range(q * step, min(K, (q + 1) * step)):
                    last = nc.scalar.activation(xneg[:, k, :], xblk[r][:, k, :], ACT.Identity,
                                                bias=neg[:, r, k:k + 1])
                if q == BITES - 1:
                    last.then_inc(neg_done, 1)

            def own_part(n, r, q):
                if q == 0:
                    act.wait_ge(mask_ready, 2 * n + r + 1)
                    act.wait_ge(blk_in[r], 16 * (n + 1))
                    act.wait_ge(neg_done, 2 * n + r + 1)
                step = -(-K // BITES)
                for k in range(q * step, min(K, (q + 1) * step)):
                    last = nc.scalar.activation(xblk[r][:, k, :], xblk[r][:, k, :], ACT.Copy,
                                                scale=mask[:, r, k:k + 1])
                if q == BITES - 1:
                    last.then_inc(own_done, 1)

            def stage_h(n, t, sums):
                act.wait_ge(xa_in, 16 * (n + 1))
                if not first(n):
                    act.wait_ge(te_T, n)
                nc.scalar.activation(xa[:, :], xa[:, :], ACT.Relu, bias=tile_of(nm, t), scale=tile_of(rs, t))
                if sums is not None:
                    act.wait_ge(added, sums)
                copy(aggs[:, :], agg[:, ds(t, 1), :].rearrange("p o d -> p (o d)"), 1.0 / HSCALE).then_inc(sc_h, 1)

            def stage_T(n):
                act.wait_ge(te_T, n + 1)
                if not first(n):
                    act.wait_ge(te_A, n)
                copy(ahT[:, :, :], pTA[:, :, :]).then_inc(sc_T, 1)

            def stage_A(n):
                act.wait_ge(te_A, n + 1)
                if not first(n):
                    act.wait_ge(te_B, 4 * n)
                for m in range(4):
                    last = nc.scalar.activation(h1T[:, m, :], pTA[:, m, :], ACT.Relu, bias=brel_c[:, m:m + 1])
                last.then_inc(sc_A, 1)

            def stage_B(n, m):
                act.wait_ge(te_B, 4 * n + m + 1)
                if m == 0 and not first(n):
                    act.wait_ge(ve_hl, n)
                for g, (row, func) in enumerate(((0, ACT.Sigmoid), (2, ACT.Tanh), (3, ACT.Sigmoid))):
                    last = nc.scalar.activation(gio[:, g, m, :], pB[m % 2][:, g, :], func,
                                                bias=gb[:, 4 * row + m:4 * row + m + 1])
                last.then_inc(sc_B, 1)

            def stage_tc(n):
                act.wait_ge(ve_c, n + 1)
                nc.scalar.activation(gio[:, 0, :, :], gio[:, 1, :, :], ACT.Tanh).then_inc(sc_tc, 1)

            def stage_T3(n):
                act.wait_ge(te_T3, n + 1)
                if not first(n):
                    act.wait_ge(te_D, 2 * n)
                copy(featT[:, :, :], pT23[0:F, 0:3 * P].rearrange("p (c n) -> p c n", c=3)).then_inc(sc_T3, 1)

            def stage_h2(n):
                act.wait_ge(ve_ln, n + 1)
                if not first(n):
                    act.wait_ge(te_T2, n)
                nc.scalar.activation(h2[:, :], x2[:, :], ACT.Relu, bias=nm2[:, :], scale=rs2[:, :]).then_inc(sc_h2, 1)

            def stage_T2(n):
                act.wait_ge(te_T2, n + 1)
                if not first(n):
                    act.wait_ge(te_D, 2 * n)
                copy(h2T[:, :, :], pT2.rearrange("p (k n) -> p k n", k=2)).then_inc(sc_T2, 1)

            def stage_D(n, g):
                act.wait_ge(te_D, 2 * n + g + 1)
                if g == 0 and not first(n):
                    act.wait_ge(te_E, n)
                for m in range(4):
                    last = nc.scalar.activation(zT[:, 4 * g + m, :], pB[g][:, m, :], ACT.Relu,
                                                bias=b1_c[:, 4 * g + m:4 * g + m + 1])
                last.then_inc(sc_D, 1)

            def body(i, units, T, B, E_):
                def second(q):
                    if T:
                        shift_block(i - 1, 1, q)

                def own(q):
                    if T:
                        own_part(i - 1, 1, q)

                def next_first(q):
                    if units:
                        shift_block(i, 0, q)

                if B:
                    stage_B(i - 2, 0)
                    stage_B(i - 2, 1)
                second(0)
                second(1)
                if T:
                    whole = PAIRS + 2 + ADDED0 if not units else ended(act, i * UPI + 1) + (i * UPI + 2 + ADDED0)
                    stage_h(i - 1, i - 1, whole)
                second(2)
                if B:
                    stage_B(i - 2, 2)
                second(3)
                if T:
                    stage_T(i - 1)
                if B:
                    stage_B(i - 2, 3)
                    stage_tc(i - 2)
                own(0)
                own(1)
                if B:
                    stage_T3(i - 2)
                own(2)
                own(3)
                if T:
                    stage_A(i - 1)
                if B:
                    stage_h2(i - 2)
                if B:
                    stage_T2(i - 2)
                next_first(0)
                next_first(1)
                if B:
                    stage_D(i - 2, 0)
                next_first(2)
                if B:
                    stage_D(i - 2, 1)
                next_first(3)

            run(act, body)

            redo = act.value_load(flags[0:1, 0:1], min_val=0, max_val=1)
            with act.If(redo):
                with act.Fori(0, NT) as t:
                    n = t + NT
                    stage_h(n, t, None)
                    stage_T(n)
                    stage_A(n)
                    for m in range(4):
                        stage_B(n, m)
                    stage_tc(n)
                    stage_T3(n)
                    stage_h2(n)
                    stage_T2(n)
                    stage_D(n, 0)
                    stage_D(n, 1)

        @block.tensor
        def _(pe):
            def mm(o, l, r, a, b):
                return nc.tensor.matmul(o, l, r, start=a, stop=b)

            pe.sem_inc(pair_done, DONE0)
            pe.wait_ge(consts, 11)
            pe.wait_ge(erow_ready, 1)
            pTf = pTA[:, :, :].rearrange("p a n -> p (a n)")
            mm(pTf[:, 0:NB], ones1, erow, True, True).then_inc(ends_ready, 1)
            pe.wait_ge(l_c, 16 * 6)
            for m in range(8):
                last = mm(pT23[:, m:m + 1], w1u[:, m * P:(m + 1) * P], u_c[:, :], True, True)
            last.then_inc(bias_mm, 1)
            pe.wait_ge(start_ready, 1)
            mm(pF[:, 0:NT], shA, start[:, 0:NT], True, False)
            mm(pF[:, 0:NT], shB, start[:, 1:NT + 1], False, True).then_inc(shifted, 1)
            mm(pB[0][:, 0, 0:NT], ones1, start[0:1, 1:NT + 1], True, True).then_inc(tile_ends, 1)
            pe.wait_ge(tcnt_ready, 1)
            for h in range(2):
                last = nc.tensor.transpose(pB[1][0:1, h, :], tcnt[:, h:h + 1], ident[:, :])
            last.then_inc(tcnt_T, 1)
            pe.wait_ge(mcnt_ready, 1)
            nc.tensor.transpose(pF[0:1, 256:256 + P], mcnt, ident[:, :]).then_inc(mcnt_T, 1)
            pe.wait_ge(tab_ready, 1)

            lo, hi, step = unit_tiles(pe)

            def pairs(u, q, v):
                with pe.Fori(lo, pe.snap(hi) + 1) as t:
                    p = pe.snap(t + u)
                    k = pe.snap(p & (RING - 1))
                    bank = pe.snap(p % BANKS)
                    pe.wait_ge(rows_in[q], 16 * J * (v + 1))
                    pe.wait_ge(hot_ready, p + 1)
                    pe.wait_ge(added, p + ADDED0)
                    for j in range(J):
                        for half in range(2):
                            last = mm(acc[:, ds(bank, 1), 0:D], hot[:, ds(k, 1), :, j],
                                      rows[q][:, j, half * D:(half + 1) * D], j + half == 0, j + half == J)
                    last.then_inc(pair_done, 1)
                step(u)

            def stage_T(n):
                pe.wait_ge(sc_h, n + 1)
                if not first(n):
                    pe.wait_ge(sc_A, n)
                for c in range(2):
                    nc.tensor.transpose(pTA[:, c, :], aggs[:, c * P:(c + 1) * P], ident[:, :])
                for c in range(2):
                    last = nc.tensor.transpose(pTA[:, 2 + c, :], xa[:, c * P:(c + 1) * P], ident[:, :])
                last.then_inc(te_T, 1)

            def stage_A(n, ms):
                pe.wait_ge(sc_T, n + 1)
                for m in ms:
                    for c in range(4):
                        w = (Wrel, Wroot)[c // 2]
                        last = mm(pTA[:, m, :], w[:, c % 2, m * P:(m + 1) * P], ahT[:, c, :], c == 0, c == 3)
                if m == 3:
                    last.then_inc(te_A, 1)

            def stage_B(n, ms):
                pe.wait_ge(sc_A, n + 1)
                for m in ms:
                    if m >= 2:
                        pe.wait_ge(sc_B, 4 * n + m - 1)
                    elif not first(n):
                        pe.wait_ge(sc_D, 2 * n - 1 + m)
                    for g in range(G3):
                        for c in range(4):
                            last = mm(pB[m % 2][:, g, :], Wih[:, c, g, m * P:(m + 1) * P], h1T[:, c, :], c == 0, c == 3)
                    last.then_inc(te_B, 1)

            def stage_FC(n):
                pe.wait_ge(ve_hl, n + 1)
                if not first(n):
                    pe.wait_ge(ve_out, n)
                for c in range(4):
                    last = mm(pFE, hlT[:, c, :], Wfc[:, c, :], c == 0, c == 3)
                last.then_inc(te_FC, 1)

            def stage_T3(n):
                pe.wait_ge(feat_ready, n + 1)
                if not first(n):
                    pe.wait_ge(sc_T2, n)
                for c in range(3):
                    last = nc.tensor.transpose(pT23[0:F, c * P:(c + 1) * P], feat[:, c, :], ident[:, :])
                last.then_inc(te_T3, 1)

            def stage_T2(n):
                pe.wait_ge(sc_h2, n + 1)
                pe.wait_ge(sc_T3, n + 1)
                for c in range(2):
                    last = nc.tensor.transpose(pT2[:, c * P:(c + 1) * P], h2[:, c * P:(c + 1) * P], ident[:, :])
                last.then_inc(te_T2, 1)

            def stage_De(n, g):
                pe.wait_ge(sc_T3, n + 1)
                pe.wait_ge(sc_B, 4 * n + 3 + g)
                for m in range(4):
                    for c in range(3):
                        mm(pB[g][:, m, :], W1e[:, c, (4 * g + m) * P:(4 * g + m + 1) * P], featT[:, c, :], m + c == 0, False)

            def stage_Dh(n, g):
                pe.wait_ge(sc_T2, n + 1)
                for m in range(4):
                    for c in range(2):
                        last = mm(pB[g][:, m, :], W1h[:, c, (4 * g + m) * P:(4 * g + m + 1) * P], h2T[:, c, :],
                                  False, m + c == 4)
                last.then_inc(te_D, 1)

            def stage_E(n):
                pe.wait_ge(sc_D, 2 * n + 2)
                pe.wait_ge(ve_x2, n + 1)
                for c in range(8):
                    last = mm(pFE, zT[:, c, :], W2[:, c, :], c == 0, c == 7)
                last.then_inc(te_E, 1)

            def body(i, units, T, B, E_):
                def pairs_of(q):
                    if units:
                        pairs(i * UPI + q, q % 2, 2 * i + q // 2)

                pairs_of(0)
                if isinstance(i, int) and i == 1:
                    pe.wait_ge(l_wa, 16 * 2)
                if isinstance(i, int) and i == 2:
                    pe.wait_ge(l_w, 16 * 9)
                if B:
                    stage_B(i - 2, (0, 1))
                if E_:
                    stage_E(i - 3)
                pairs_of(1)
                if B:
                    stage_B(i - 2, (2,))
                if T:
                    stage_T(i - 1)
                if B:
                    stage_B(i - 2, (3,))
                pairs_of(2)
                if B:
                    stage_T3(i - 2)
                if T:
                    stage_A(i - 1, (0, 1))
                if B:
                    stage_FC(i - 2)
                if T:
                    stage_A(i - 1, (2, 3))
                pairs_of(3)
                if B:
                    stage_De(i - 2, 0)
                    stage_T2(i - 2)
                    stage_De(i - 2, 1)
                    stage_Dh(i - 2, 0)
                    stage_Dh(i - 2, 1)

            run(pe, body)

            redo = pe.value_load(flags[0:1, 0:1], min_val=0, max_val=1)
            with pe.If(redo):
                with pe.Fori(0, NT) as t:
                    n = t + NT
                    stage_T(n)
                    stage_A(n, range(4))
                    stage_B(n, range(4))
                    stage_FC(n)
                    stage_T3(n)
                    stage_T2(n)
                    for g in range(2):
                        stage_De(n, g)
                        stage_Dh(n, g)
                    stage_E(n)

        @block.vector
        def _(dve):
            ts, tt, stt = nc.vector.tensor_scalar, nc.vector.tensor_tensor, nc.vector.scalar_tensor_tensor
            copy, reduce = nc.vector.tensor_copy, nc.vector.tensor_reduce

            def chain(sem_, count):
                def link(ins, meanwhile=None):
                    nonlocal count
                    count = count + 1
                    ins.then_inc(sem_, 1)
                    if meanwhile is not None:
                        meanwhile()
                    dve.wait_ge(sem_, count)
                return link

            pro = chain(pd, 0)

            def rstd(link, y, var, v, s):
                link(ts(v, var, EPS, None, ALU.add))
                link(ts(s.bitcast(i32), v.bitcast(i32), 1, None, ALU.logical_shift_right))
                link(ts(y.bitcast(i32), s.bitcast(i32), -1.0, float(0x5F3759DF), ALU.mult, ALU.add))
                link(ts(v, v, -0.5, None, ALU.mult))
                for _ in range(3):
                    if y.shape[1] == 1:
                        link(stt(s, y, v, y, ALU.mult, ALU.mult))
                    else:
                        link(tt(s, y, y, ALU.mult))
                        link(tt(s, s, v, ALU.mult))
                    link(stt(y, s, 1.5, y, ALU.add, ALU.mult))

            dve.wait_ge(l_e, 16)
            copy(erow, erow_i).then_inc(erow_ready, 1)
            dve.wait_ge(ends_ready, 1)
            pro(copy(ends_b, pTA[:, :, :].rearrange("p a n -> p (a n)")[:, 0:NB]))
            dve.wait_ge(consts, 11)

            def coarse(t):
                return ts(junk[t % LNG][:, 0:NB // 2].bitcast(i16), ends_b, node[:, t:t + 1], 0.0, ALU.is_lt, ALU.add,
                          accum_out=blk[:, t:t + 1])

            def coarse_out(g):
                w = slice(g * LNG, (g + 1) * LNG)
                pro(ts(blk[:, w], blk[:, w], float(NB - 1), None, ALU.min))
                copy(blku[:, w], blk[:, w]).then_inc(coarse_ready, LNG)

            def place(t):
                dve.wait_ge(fine_in[t % SLOTS], 16 * (t // SLOTS + 1))
                ts(junk[t % LNG], fine[t % SLOTS], node[:, t:t + 1], 0.0, ALU.is_lt, ALU.add,
                   accum_out=start[:, t:t + 1]).then_inc(fine_used, 1)

            def norm(g):
                w = slice(g * LNG, (g + 1) * LNG)
                step = 0

                def search():
                    if step < LNG and g + 1 < NT // LNG:
                        coarse((g + 1) * LNG + step)
                    elif LNG <= step < 2 * LNG and g >= 1:
                        place((g - 1) * LNG + step - LNG)

                def spaced(ins):
                    nonlocal step
                    pro(ins, search)
                    step += 1

                dve.wait_ge(l_x[g % 2], 16 * (g // 2 + 1))
                for t in range(LNG):
                    last = nc.vector.bn_stats(st[:, t, :], xg[g % 2][:, t, :])
                pro(last)
                for t in range(LNG):
                    last = nc.vector.bn_aggr(mv[:, t, :], st[:, t, :])
                spaced(last)
                rstd(spaced, rs[:, w], mv[:, :, 1], lna[:, :], lnb[:, :])
                spaced(stt(nm[:, w], mv[:, :, 0], -1.0, rs[:, w], ALU.mult, ALU.mult))
                assert step >= 2 * LNG
                ts(rs_s[:, w], rs[:, w], HSCALE, None, ALU.mult)
                ts(nm_s[:, w], nm[:, w], HSCALE, None, ALU.mult).then_inc(ln_stats, 1)
                if g + 1 < NT // LNG:
                    coarse_out(g + 1)
                if g >= 1:
                    dve.wait_ge(fine_used, LNG * g)

            for t in range(LNG):
                last = coarse(t)
            pro(last)
            coarse_out(0)
            for g in range(NT // LNG):
                norm(g)
            for t in range(NT - LNG, NT):
                place(t)
            dve.wait_ge(fine_used, NT)

            pro(nc.vector.memset(start[:, NT:NT + 1], float(E)))
            pro(stt(start[:, 0:NT], blk[:, :], float(SB), start[:, 0:NT], ALU.mult, ALU.add))
            dve.sem_inc(start_ready, 1)
            dve.wait_ge(l_d, 16)
            copy(dtab[:, :], d32)
            dve.wait_ge(l_c, 16 * 6)
            tt(gb[:, :], gb[:, :], gb2[:, :], ALU.add)
            dve.wait_ge(bias_mm, 1)
            tt(b1_c[:, :], b1_c[:, :], pT23[:, 0:8], ALU.add)
            dve.wait_ge(tile_ends, 1)
            for h in range(2):
                last = ts(junk[h][:, 0:NT], pB[0][:, 0, 0:NT], lim[:, h:h + 1], 0.0, ALU.is_le, ALU.add,
                          accum_out=tcnt[:, h:h + 1])
            last.then_inc(tcnt_ready, 1)
            dve.wait_ge(shifted, 1)
            pro(copy(end[:, :], pF[:, 0:NT]))
            pro(tt(cntt, end[:, :], start[:, 0:NT], ALU.subtract))
            reduce(mcnt, cntt, AX.X, ALU.max).then_inc(mcnt_ready, 1)
            dve.wait_ge(ln_h, NT // LNG)
            ts(hasany[:, :], cntt, 0.0, None, ALU.is_gt)
            pro(ts(rcnt[:, :], cntt, 1.0, None, ALU.max))
            pro(nc.vector.reciprocal(rcnt[:, :], rcnt[:, :]))
            for r in range(NR):
                s, far = cntt, rcnt_tmp
                pro(ts(s, start[:, 0:NT], float(K * r), None, ALU.add))
                pro(ts(browf, s, float(E - K), None, ALU.min))
                pro(tt(blo[:, r, :], s, browf, ALU.subtract))
                pro(tt(bhi[:, r, :], end[:, :], browf, ALU.subtract))
                pro(tt(far, s, end[:, :], ALU.is_ge))
                pro(stt(browf, far, FAR, browf, ALU.mult, ALU.add))
                pro(copy(brow[:, r, :], browf))
            tile_end = start[0:1, 1:NT + 1]
            nc.vector.memset(tab[:, 0:1], 0)
            nc.vector.memset(tab[:, NU + 1:NU + 2], 0)
            dve.wait_ge(tcnt_T, 1)
            pro(copy(tab[:, 1:NU + 1].rearrange("o (p h) -> o h p", h=2), pB[1][0:1, 0:2, 0:NU // 2]))
            pro(ts(limt, base[0:1, 1:NT + 1], float(UPI * UNIT // P), float(UNIT), ALU.mult, ALU.add))
            pro(tt(cmpt, tile_end, limt, ALU.is_gt))
            dve.wait_ge(mcnt_T, 1)
            pro(reduce(fl[:, 0:1], cmpt, AX.X, ALU.max))
            pro(reduce(fl[:, 1:2], pF[0:1, 256:256 + P], AX.X, ALU.max))
            pro(ts(fl[:, 2:3], fl[:, 1:2], float(NR * K), None, ALU.is_gt))
            pro(tt(fl[:, 0:1], fl[:, 0:1], fl[:, 2:3], ALU.max))
            pro(copy(flags[:, :], fl[:, 0:2]))
            for b in range(BANKS):
                last = nc.vector.memset(acc[:, b, :], 0.0)
            last.then_inc(added, 1)
            dve.wait_ge(zeroed, 1)

            def masks(n, r):
                link = chain(mchain, (n * NR + r) * 2)
                link(ts(mask[:, r, :], col[:, 0:K], tile_of(blo[:, r, :], n), None, ALU.is_ge))
                link(stt(mask[:, r, :], col[:, 0:K], tile_of(bhi[:, r, :], n), mask[:, r, :], ALU.is_lt, ALU.mult))
                ts(neg[:, r, :], mask[:, r, :], 1.0, BIG, ALU.subtract, ALU.mult).then_inc(mask_ready, 1)

            dve.sem_inc(tab_ready, 1)

            lo, hi, step = unit_tiles(dve)
            one, two = dve.alloc_register("tile_one_back"), dve.alloc_register("tile_two_back")
            dve.reg_mov(one, NT)
            dve.reg_mov(two, NT)

            def add_sums(p):
                dve.wait_ge(pair_done, p + (DONE0 - 1))
                dve.wait_ge(added, p + ADDED0)
                to = agg[:, ds(dve.snap(two), 1), :]
                tt(to, to, acc[:, ds((p + 1) % BANKS, 1), 0:D], ALU.add).then_inc(added, 1)

            def pairs(u):
                with dve.Fori(lo, dve.snap(hi) + 1) as t:
                    p = dve.snap(t + u)
                    dve.wait_ge(pair_done, p + 1)
                    k = dve.snap(p & (RING - 1))
                    ts(drel[:, ds(k, 1), :], dtab[:, ds(u * J, J)], tile_of(base, t), None, ALU.subtract
                       ).then_inc(drel_ready, 1)
                    dve.wait_ge(drel_ready, p + 1)
                    tt(hot[:, ds(k, 1), :, :].rearrange("p o n j -> p (o n) j"), col8[:, :, :],
                       drel[:, ds(k, 1), :].to_broadcast([P, P, J]), ALU.is_equal).then_inc(hot_ready, 1)
                    add_sums(p)
                    dve.reg_mov(two, one)
                    dve.reg_mov(one, t)
                step(u)

            def block_max(n, r):
                dve.wait_ge(neg_done, 2 * n + r + 1)
                reduce(part[:, r, 1, :], xneg[:, :, :].rearrange("p k f -> p f k"), AX.X, ALU.max).then_inc(neg_used, 1)

            def block_own(n, r):
                chain(fchain, n)(
                    tt(xblk[r][:, :, :], xblk[r][:, :, :], mask[:, r, :].unsqueeze(2).to_broadcast([P, K, F]), ALU.mult))

            def block_sum(n, r):
                reduce(part[:, r, 0, :], xblk[r][:, :, :].rearrange("p k f -> p f k"), AX.X, ALU.add).then_inc(blk_used[r], 1)

            def features(link, n, t, s, m):
                if not first(n):
                    dve.wait_ge(te_T3, n)
                link(ts(feat[:, 1, :], m, tile_of(hasany, t), None, ALU.mult))
                copy(feat[:, 0, :], s)
                ts(feat[:, 2, :], s, tile_of(rcnt, t), None, ALU.mult).then_inc(feat_ready, 1)

            def combine(n, t):
                link = chain(rchain, n * 3)
                dve.wait_ge(neg_used, 2 * n + 2)
                link(tt(part[:, 0, 1, :], part[:, 0, 1, :], part[:, 1, 1, :], ALU.max))
                link(tt(part[:, 0, 0, :], part[:, 0, 0, :], part[:, 1, 0, :], ALU.add))
                features(link, n, t, part[:, 0, 0, :], part[:, 0, 1, :])

            def stage_c(n):
                dve.wait_ge(sc_B, 4 * n + 4)
                tt(gio[:, 1, :, :], gio[:, 0, :, :], gio[:, 1, :, :], ALU.mult).then_inc(ve_c, 1)
                dve.wait_ge(sc_tc, n + 1)
                if not first(n):
                    dve.wait_ge(te_FC, n)
                tt(hlT[:, :, :], gio[:, 0, :, :], gio[:, 2, :, :], ALU.mult).then_inc(ve_hl, 1)

            def stage_LN(n):
                link = chain(lchain, n * 14)
                dve.wait_ge(te_FC, n + 1)
                dve.wait_ge(xf_in, 16 * (n + 1))
                tt(x2[:, :], pFE, xf[:, :], ALU.add).then_inc(ve_x2, 1)
                dve.wait_ge(ve_x2, n + 1)
                link(tt(x2[:, :], x2[:, :], bfc_r[:, :], ALU.add))
                link(nc.vector.bn_stats(st[:, 0, :], x2[:, :]))
                alone(dve)
                link(nc.vector.bn_aggr(mv[:, 0, :], st[:, 0, :]))
                rstd(link, rs2[:, :], mv[:, 0, 1:2], lna[:, 0:1], lnb[:, 0:1])
                link(stt(nm2[:, :], mv[:, 0, 0:1], -1.0, rs2[:, :], ALU.mult, ALU.mult))
                dve.sem_inc(ve_ln, 1)

            def stage_res(n):
                link = chain(schain, n)
                dve.wait_ge(sc_h2, n + 1)
                link(tt(x2[:, :], x2[:, :], h2[:, :], ALU.add))
                tt(x2[:, :], x2[:, :], b2_r[:, :], ALU.add).then_inc(ve_res, 1)

            def stage_out(n):
                dve.wait_ge(te_E, n + 1)
                dve.wait_ge(ve_res, n + 1)
                if not first(n):
                    dve.wait_ge(stored, 16 * n)
                tt(ob[:, :], pFE, x2[:, :], ALU.add).then_inc(ve_out, 1)

            def body(i, units, T, B, E_):
                whole_loop = not (isinstance(i, int) and i == NT - 1)

                def pairs_ahead(q):
                    if units and (q < UPI or whole_loop):
                        pairs(i * UPI + q)
                    elif units:
                        add_sums(PAIRS)
                        dve.reg_mov(two, one)
                        add_sums(PAIRS + 1)

                if T:
                    block_max(i - 1, 0)
                pairs_ahead(1)
                if T:
                    block_own(i - 1, 0)
                    block_sum(i - 1, 0)
                pairs_ahead(2)
                if E_:
                    stage_out(i - 3)
                if units:
                    masks(i, 0)
                if B:
                    stage_c(i - 2)
                pairs_ahead(3)
                if B:
                    stage_LN(i - 2)
                if T:
                    block_max(i - 1, 1)
                    dve.wait_ge(own_done, i)
                    block_sum(i - 1, 1)
                pairs_ahead(4)
                if T:
                    combine(i - 1, i - 1)
                if B:
                    stage_res(i - 2)
                if units:
                    masks(i, 1)

            pairs(0)
            run(dve, body)

            redo = dve.value_load(flags[0:1, 0:1], min_val=0, max_val=1)
            most = dve.value_load(flags[0:1, 1:2], min_val=0, max_val=E)
            with dve.If(redo):
                n_link, n_blk = dve.alloc_register("redo_links"), dve.alloc_register("redo_blocks_v")
                dve.reg_mov(n_link, 0)
                dve.reg_mov(n_blk, 0)

                def link(ins):
                    ins.then_inc(rdchain, 1)
                    dve.reg_add(n_link, n_link, 1)
                    dve.wait_ge(rdchain, n_link)

                s, m = part[:, 0, 0, :], part[:, 0, 1, :]
                own, off = neg[:, 0, :], neg[:, 1, :]
                row, lo, hi, far = (rx[:, q:q + 1] for q in range(4))
                nxt = rx[:, 4:5]
                with dve.Fori(0, NT) as t:
                    link(nc.vector.memset(s, 0.0))
                    link(nc.vector.memset(m, -BIG))
                    link(copy(nxt, tile_of(start, t)))
                    alone(dve)
                    with dve.Fori(0, most, K):
                        link(ts(row, nxt, float(E - K), None, ALU.min))
                        link(tt(lo, nxt, row, ALU.subtract))
                        link(tt(hi, tile_of(end, t), row, ALU.subtract))
                        link(tt(far, nxt, tile_of(end, t), ALU.is_ge))
                        link(stt(row, far, FAR, row, ALU.mult, ALU.add))
                        link(copy(rxu, row))
                        dve.sem_inc(r_idx, 1)
                        link(ts(nxt, nxt, float(K), None, ALU.add))
                        link(ts(own, col[:, 0:K], lo, None, ALU.is_ge))
                        link(stt(own, col[:, 0:K], hi, own, ALU.is_lt, ALU.mult))
                        link(ts(off, own, 1.0, BIG, ALU.subtract, ALU.mult))
                        dve.reg_add(n_blk, n_blk, 1)
                        dve.wait_ge(r_clear, n_blk)
                        dve.wait_ge(r_in, 16)
                        blk_ = xblk[0][:, :, :]
                        link(tt(xneg[:, :, :], blk_, own.unsqueeze(2).to_broadcast([P, K, F]), ALU.mult))
                        link(reduce(part[:, 1, 0, :], xneg[:, :, :].rearrange("p k f -> p f k"), AX.X, ALU.add))
                        link(tt(s, s, part[:, 1, 0, :], ALU.add))
                        link(tt(xneg[:, :, :], blk_, off.unsqueeze(2).to_broadcast([P, K, F]), ALU.add))
                        link(reduce(part[:, 1, 1, :], xneg[:, :, :].rearrange("p k f -> p f k"), AX.X, ALU.max))
                        link(tt(m, m, part[:, 1, 1, :], ALU.max))
                        alone(dve)
                    n = t + NT
                    features(link, n, t, s, m)
                    stage_c(n)
                    stage_LN(n)
                    stage_res(n)
                    stage_out(n)


def kernel(**inputs):
    import numpy as np
    import concourse.bacc as bacc
    from concourse.bass_utils import run_bass_kernel_spmd

    a = {k: np.asarray(v) for k, v in inputs.items()}

    def padded(v, n, fill):
        o = np.full((n,) + v.shape[1:], fill, v.dtype)
        o[:v.shape[0]] = v
        return o

    def by_partition(v):
        return np.ascontiguousarray(v.reshape(-1, P).T)

    arrays = {
        "x": padded(a["x"], NPAD, 0),
        "src": padded(a["src"], EPAD, 0).reshape(EPAD, 1),
        "dst": padded(a["dst"], EPAD, NPAD + P),
        "edge": np.ascontiguousarray(a["edge_attr_96"]),
        "wrel": np.ascontiguousarray(a["L0_gnn_W_rel"]),
        "brel": by_partition(a["L0_gnn_b_rel"]),
        "wroot": np.ascontiguousarray(a["L0_gnn_W_root"]),
        "wih": np.ascontiguousarray(a["L0_gnn_W_ih"].T),
        "bih": by_partition(a["L0_gnn_b_ih"]),
        "bhh": by_partition(a["L0_gnn_b_hh"]),
        "wfc": np.ascontiguousarray(a["L0_gnn_W_fc"]),
        "bfc": a["L0_gnn_b_fc"].reshape(1, D),
        "u0": np.ascontiguousarray(a["L1_gnn_u"][0].reshape(-1, 1)),
        "w1": np.ascontiguousarray(a["L1_gnn_W1"]),
        "b1": by_partition(a["L1_gnn_b1"]),
        "w2": np.ascontiguousarray(a["L1_gnn_W2"]),
        "b2": a["L1_gnn_b2"].reshape(1, D),
    }
    nc = bacc.Bacc("TRN2", target_bir_lowering=False, num_devices=1, dynamic_dma_scratch_size=8192)
    args = [nc.dram_tensor(f"in_{k}", v.shape, mybir.dt.uint32 if k == "src" else mybir.dt.from_np(v.dtype),
                           kind="ExternalInput").ap() for k, v in arrays.items()]
    out = nc.dram_tensor("out", (NPAD, D), mybir.dt.float32, kind="ExternalOutput").ap()
    build(nc, *args, out)
    r = run_bass_kernel_spmd(nc, [{f"in_{k}": v.view(np.uint32) if k == "src" else v for k, v in arrays.items()}],
                             core_ids=[0])
    return r.results[0]["out"][:N]
```
